# Optimizing a Trainium2 kernel written in Bass

```python
import numpy as np
import jax
import jax.numpy as jnp

def _softmax(x, axis=-1):
    return jax.nn.softmax(x, axis=axis)

def _gelu(x):
    return jax.nn.gelu(x, approximate=True)

def _silu(x):
    return jax.nn.silu(x)

def _sigmoid(x):
    return jax.nn.sigmoid(x)

def _layernorm(x, axis=-1, eps=1e-05):
    m = jnp.mean(x, axis=axis, keepdims=True)
    v = jnp.var(x, axis=axis, keepdims=True)
    return (x - m) / jnp.sqrt(v + eps)

def _scatter_add(tgt, idx, src, axis=0):
    return tgt.at[idx].add(src)

def _segment_sum(src, seg, n):
    return jax.ops.segment_sum(src, seg, n)
kernel_name = 'mk_adj_resnorm_d2_adj_r2_60d248'

def setup_inputs(seed: int=0):
    np.random.seed(seed)
    _w = jnp.asarray

    def _rec_inputs():
        import jax
        import jax.numpy as jnp
        _gk = jax.random.key(seed)
        x = 7.22e-05 + 1 * jax.random.normal(jax.random.fold_in(_gk, 1), (32, 256, 128), jnp.float32)
        _w = (1.0 + jnp.arange(256, dtype=jnp.float32)) ** (-0.5)
        _w = _w / _w.mean()
        _pij = jnp.clip(0.0625 * _w[:, None] * _w[None, :], 0.0, 1.0)
        _a = jax.random.uniform(jax.random.fold_in(_gk, 2), (32, 256, 256)) < _pij
        _a = jnp.logical_or(_a, jnp.swapaxes(_a, -1, -2))
        _a = jnp.logical_or(_a, jnp.eye(256, dtype=bool))
        _af = _a.astype(jnp.float32)
        adj = _af
        return (x, adj)
    x, adj = _rec_inputs()

    def _L0_gnn_setup():
        import jax, jax.numpy as jnp
        import numpy as np
        from jax import lax
        DIM = 128
        EPS = 1e-05

        def _bn(h, g, b, m, v):
            scale = g / jnp.sqrt(v + EPS)
            return h * scale[None, :, None] + (b - m * scale)[None, :, None]

        def _conv1d(h, w, pad):
            return lax.conv_general_dilated(h, w, window_strides=(1,), padding=[(pad, pad)], dimension_numbers=('NCH', 'OIH', 'NCH'))
        key = jax.random.key(seed)
        ks = jax.random.split(key, 16)
        bs, n, d = (16, 1024, DIM)
        s = 0.05
        return {'x': jax.random.normal(ks[0], (bs, n, d), jnp.float32), 'mask': jnp.ones((bs, n, n), jnp.float32), 'w_se': jax.random.normal(ks[1], (3, d), jnp.float32) * s, 'b_se': jnp.zeros((3,), jnp.float32), 'conv1_w': jax.random.normal(ks[2], (d, d, 1), jnp.float32) * s, 'bn1_g': jnp.ones((d,), jnp.float32), 'bn1_b': jnp.zeros((d,), jnp.float32), 'bn1_m': jnp.zeros((d,), jnp.float32), 'bn1_v': jnp.ones((d,), jnp.float32), 'conv2_w': jax.random.normal(ks[3], (d, d, 17), jnp.float32) * s, 'bn2_g': jnp.ones((d,), jnp.float32), 'bn2_b': jnp.zeros((d,), jnp.float32), 'bn2_m': jnp.zeros((d,), jnp.float32), 'bn2_v': jnp.ones((d,), jnp.float32), 'w_msg': jax.random.normal(ks[4], (d, d), jnp.float32) * s, 'b_msg': jnp.zeros((d,), jnp.float32), 'w_ih': jax.random.normal(ks[5], (3 * d, 2 * d), jnp.float32) * s, 'b_ih': jnp.zeros((3 * d,), jnp.float32), 'w_hh': jax.random.normal(ks[6], (3 * d, d), jnp.float32) * s, 'b_hh': jnp.zeros((3 * d,), jnp.float32)}
    _L0_gnn_all = _L0_gnn_setup()
    _L0_gnn_in = {k: v for k, v in _L0_gnn_all.items() if k in ('w_se', 'b_se', 'conv1_w', 'bn1_g', 'bn1_b', 'bn1_m', 'bn1_v', 'conv2_w', 'bn2_g', 'bn2_b', 'bn2_m', 'bn2_v', 'w_msg', 'b_msg', 'w_ih', 'b_ih', 'w_hh', 'b_hh')}
    del _L0_gnn_all

    def _L1_gnn_setup():
        import jax, jax.numpy as jnp
        import numpy as np
        D_IN = 128
        D_HID = 256
        key = jax.random.key(seed)
        k1, k2, k3, k4, k5, k6 = jax.random.split(key, 6)
        x = jax.random.normal(k1, (8, 2048, D_IN), dtype=jnp.float32)
        adj = jax.random.uniform(k2, (8, 2048, 2048), dtype=jnp.float32)
        s1 = 1.0 / np.sqrt(D_IN)
        s2 = 1.0 / np.sqrt(D_HID)
        W1 = jax.random.uniform(k3, (D_IN, D_HID), dtype=jnp.float32, minval=-s1, maxval=s1)
        b1 = jax.random.uniform(k4, (D_HID,), dtype=jnp.float32, minval=-s1, maxval=s1)
        W2 = jax.random.uniform(k5, (D_HID, D_IN), dtype=jnp.float32, minval=-s2, maxval=s2)
        b2 = jax.random.uniform(k6, (D_IN,), dtype=jnp.float32, minval=-s2, maxval=s2)
        eps = jnp.zeros((1,), dtype=jnp.float32)
        return {'x': x, 'adj': adj, 'eps': eps, 'W1': W1, 'b1': b1, 'W2': W2, 'b2': b2}
    _L1_gnn_all = _L1_gnn_setup()
    _L1_gnn_in = {k: v for k, v in _L1_gnn_all.items() if k in ('eps', 'W1', 'b1', 'W2', 'b2')}
    del _L1_gnn_all
    return {'x': x, 'adj': adj, 'L0_gnn_w_se': _L0_gnn_in['w_se'], 'L0_gnn_b_se': _L0_gnn_in['b_se'], 'L0_gnn_conv1_w': _L0_gnn_in['conv1_w'], 'L0_gnn_bn1_g': _L0_gnn_in['bn1_g'], 'L0_gnn_bn1_b': _L0_gnn_in['bn1_b'], 'L0_gnn_bn1_m': _L0_gnn_in['bn1_m'], 'L0_gnn_bn1_v': _L0_gnn_in['bn1_v'], 'L0_gnn_conv2_w': _L0_gnn_in['conv2_w'], 'L0_gnn_bn2_g': _L0_gnn_in['bn2_g'], 'L0_gnn_bn2_b': _L0_gnn_in['bn2_b'], 'L0_gnn_bn2_m': _L0_gnn_in['bn2_m'], 'L0_gnn_bn2_v': _L0_gnn_in['bn2_v'], 'L0_gnn_w_msg': _L0_gnn_in['w_msg'], 'L0_gnn_b_msg': _L0_gnn_in['b_msg'], 'L0_gnn_w_ih': _L0_gnn_in['w_ih'], 'L0_gnn_b_ih': _L0_gnn_in['b_ih'], 'L0_gnn_w_hh': _L0_gnn_in['w_hh'], 'L0_gnn_b_hh': _L0_gnn_in['b_hh'], 'L1_gnn_eps': _L1_gnn_in['eps'], 'L1_gnn_W1': _L1_gnn_in['W1'], 'L1_gnn_b1': _L1_gnn_in['b1'], 'L1_gnn_W2': _L1_gnn_in['W2'], 'L1_gnn_b2': _L1_gnn_in['b2']}

def reference(x, adj, L0_gnn_w_se, L0_gnn_b_se, L0_gnn_conv1_w, L0_gnn_bn1_g, L0_gnn_bn1_b, L0_gnn_bn1_m, L0_gnn_bn1_v, L0_gnn_conv2_w, L0_gnn_bn2_g, L0_gnn_bn2_b, L0_gnn_bn2_m, L0_gnn_bn2_v, L0_gnn_w_msg, L0_gnn_b_msg, L0_gnn_w_ih, L0_gnn_b_ih, L0_gnn_w_hh, L0_gnn_b_hh, L1_gnn_eps, L1_gnn_W1, L1_gnn_b1, L1_gnn_W2, L1_gnn_b2):
    import jax
    import jax.numpy as jnp

    def _L0_gnn_ref(x, mask, w_se, b_se, conv1_w, bn1_g, bn1_b, bn1_m, bn1_v, conv2_w, bn2_g, bn2_b, bn2_m, bn2_v, w_msg, b_msg, w_ih, b_ih, w_hh, b_hh):
        import jax, jax.numpy as jnp
        import numpy as np
        from jax import lax
        DIM = 128
        EPS = 1e-05

        def _bn(h, g, b, m, v):
            scale = g / jnp.sqrt(v + EPS)
            return h * scale[None, :, None] + (b - m * scale)[None, :, None]

        def _conv1d(h, w, pad):
            return lax.conv_general_dilated(h, w, window_strides=(1,), padding=[(pad, pad)], dimension_numbers=('NCH', 'OIH', 'NCH'))
        d = x.shape[-1]
        xc = jnp.transpose(x, (0, 2, 1))
        h = _bn(_conv1d(xc, conv1_w, 0), bn1_g, bn1_b, bn1_m, bn1_v)
        h = jax.nn.relu(h)
        h = _bn(_conv1d(h, conv2_w, 8), bn2_g, bn2_b, bn2_m, bn2_v)
        x_conv = jnp.transpose(jax.nn.relu(h + xc), (0, 2, 1))
        s = x @ w_se.T + b_se
        sq = jnp.sum(s * s, axis=-1)
        dist = sq[:, :, None] + sq[:, None, :] - 2.0 * jnp.einsum('bnd,bmd->bnm', s, s)
        A = jnp.exp(-dist) * mask
        msg = jax.nn.relu(x @ w_msg.T + b_msg)
        x_nmp = jnp.einsum('bnm,bmd->bnd', A, msg)
        x_in = jnp.concatenate([x_conv, x_nmp], axis=-1)
        gi = x_in @ w_ih.T + b_ih
        gh = x @ w_hh.T + b_hh
        gi_r, gi_z, gi_n = (gi[..., :d], gi[..., d:2 * d], gi[..., 2 * d:])
        gh_r, gh_z, gh_n = (gh[..., :d], gh[..., d:2 * d], gh[..., 2 * d:])
        r = jax.nn.sigmoid(gi_r + gh_r)
        z = jax.nn.sigmoid(gi_z + gh_z)
        nn_ = jnp.tanh(gi_n + r * gh_n)
        return (1.0 - z) * nn_ + z * x

    def _L1_gnn_ref(x, adj, eps, W1, b1, W2, b2):
        import jax, jax.numpy as jnp
        import numpy as np
        D_IN = 128
        D_HID = 256
        aggregated = jnp.einsum('bnm,bmd->bnd', adj, x)
        h = (1.0 + eps) * x + aggregated
        h = jax.nn.relu(h @ W1 + b1)
        return h @ W2 + b2
    x = _layernorm(x + _L0_gnn_ref(x, adj, L0_gnn_w_se, L0_gnn_b_se, L0_gnn_conv1_w, L0_gnn_bn1_g, L0_gnn_bn1_b, L0_gnn_bn1_m, L0_gnn_bn1_v, L0_gnn_conv2_w, L0_gnn_bn2_g, L0_gnn_bn2_b, L0_gnn_bn2_m, L0_gnn_bn2_v, L0_gnn_w_msg, L0_gnn_b_msg, L0_gnn_w_ih, L0_gnn_b_ih, L0_gnn_w_hh, L0_gnn_b_hh), axis=-1)
    x = _layernorm(x + _L1_gnn_ref(x, adj, L1_gnn_eps, L1_gnn_W1, L1_gnn_b1, L1_gnn_W2, L1_gnn_b2), axis=-1)
    return x

_drawn_inputs = setup_inputs


def setup_inputs(seed=0):
    import zlib

    import numpy as np

    out = dict(_drawn_inputs(seed))
    spreads = {'L0_gnn_b_se': (0.0, 0.8),
     'L0_gnn_bn1_g': (1.0, 0.6),
     'L0_gnn_bn1_b': (0.0, 0.37),
     'L0_gnn_bn1_m': (0.0, 0.351),
     'L0_gnn_bn1_v': (1.0, 0.6),
     'L0_gnn_bn2_g': (1.0, 0.2),
     'L0_gnn_bn2_b': (0.0, 0.537),
     'L0_gnn_bn2_m': (0.0, 0.459),
     'L0_gnn_bn2_v': (1.0, 0.6),
     'L0_gnn_b_msg': (0.0, 0.1),
     'L0_gnn_b_ih': (0.0, 0.1),
     'L0_gnn_b_hh': (0.0, 0.1)}
    factors = {'L1_gnn_b1': 5.625, 'L1_gnn_b2': 2.809}
    for name, (base, spread) in spreads.items():
        noise = np.random.default_rng([zlib.crc32(name.encode()), seed]).standard_normal(out[name].shape)
        drawn = base * np.exp(spread * noise) if base else spread * noise
        out[name] = jnp.asarray(drawn.astype(out[name].dtype))
    for name, factor in factors.items():
        out[name] = (out[name] * factor).astype(out[name].dtype)
    return out
```

```python
import concourse.bass as bass
from concourse import mybir
from contextlib import ExitStack
import numpy as np

B, N, D = 32, 256, 128
TAPS = 17
HID = 256
NSE = 3
EPS = 1e-5

GB = 4
GROUPS = B // GB
P = 128
PAR = N // P
T = N // PAR
PAIRS = GB // 2
COLS = GB * N
PC = COLS // PAIRS
BLK = PC // P
PAD = (TAPS // 2) // PAR
TL = T + 2 * PAD
NM, NP_, NR = (TAPS + 1) // 2, (TAPS + 1) // 2, TAPS // 2

SLOT = {("conv1", 0): 0}
for _k in range(NM):
    SLOT[("M", _k)] = len(SLOT)
for _k in range(NP_):
    SLOT[("A", _k)] = len(SLOT)
for _k in range(NR):
    SLOT[("B", _k)] = len(SLOT)
for _gate in range(3):
    for _src in ("conv", "nmp", "hid"):
        SLOT[(_src, _gate)] = len(SLOT)
NSLOT = len(SLOT)
SB = 4
assert NSLOT % SB == 0

(BN1_G, BN1_B, BN1_M, BN1_V, BN2_G, BN2_B, BN2_M, BN2_V,
 BIH, BHH, B1) = 0, 1, 2, 3, 4, 5, 6, 7, 8, 11, 14
NVEC = 16

SROWS = 96
SQ_MASK, LIN_ONE, A_MUL, A_ADD, B_MUL, B_ADD = range(6)


def shape_constants():
    c = np.zeros((P, P + 6), np.float32)
    c[:, :P] = np.eye(P, dtype=np.float32)
    for q in range(3):
        for j in range(3):
            for i in range(NSE):
                r = 32 * q + NSE * j + i
                c[r, P + SQ_MASK] = j > 0
                c[r, P + LIN_ONE] = j == 0
                c[r, P + A_MUL] = (2.0, 0.0, 1.0)[j]
                c[r, P + A_ADD] = -1.0 if j == 1 and q != 0 else 0.0
                c[r, P + B_MUL] = (1.0, 1.0, 0.0)[j]
                c[r, P + B_ADD] = -1.0 if j == 2 and q != 2 else 0.0
    return c


def gnn_kernel(nc, t, out):
    fp32 = mybir.dt.float32
    f32r = mybir.dt.float32r
    ALU = mybir.AluOpType
    ACT = mybir.ActivationFunctionType

    x_v = t["x"].rearrange("(g b) (t r) d -> g t b (r d)", b=GB, r=PAR)
    adj_v = t["adj"].rearrange("(g b) (t r) m -> g t b (r m)", b=GB, r=PAR)
    out_v = out.rearrange("(g h b) (t r) d -> g h t b (r d)", h=PAIRS, b=GB // PAIRS, r=PAR)

    ctx = ExitStack()
    with ctx:
        def sb(name, shape, dt=fp32):
            return ctx.enter_context(nc.sbuf_tensor(name, shape, dt))

        def sem(name):
            return ctx.enter_context(nc.semaphore(name))

        cst = sb("cst", [P, P + 6])
        ident = cst[:, 0:P]
        vrows = sb("vrows", [NVEC, P])
        vec = sb("vec", [P, NVEC])
        bn = sb("bn", [P, 8])
        gbias = sb("gbias", [P, 4])
        minus_half = sb("minus_half", [P, BLK])
        epst = sb("epst", [P, 2, BLK])
        epscol = sb("epscol", [P, 1])
        diag = sb("diag", [P, P])
        bmsg = sb("bmsg", [P, P])
        b2bc = sb("b2bc", [P, P])
        wmsgT = sb("wmsgT", [P, P])
        w2 = sb("w2", [P, HID // P, D])
        wh = sb("wh", [P, NSLOT, P], f32r)
        wl = sb("wl", [P, NSLOT, P], f32r)
        w1h = sb("w1h", [P, HID], f32r)
        w1l = sb("w1l", [P, HID], f32r)
        wseh = sb("wseh", [P, SROWS], f32r)
        wsel = sb("wsel", [P, SROWS], f32r)
        serows = sb("serows", [SROWS, P + 1])
        sescale = sb("sescale", [SROWS, 1])

        x_tok = sb("x_tok", [P, GB, PAR, D])
        adj_tok = sb("adj_tok", [P, GB, PAR, N])
        xv = [sb(f"xv{i}", [P, COLS]) for i in range(2)]
        xh = [sb(f"xh{i}", [P, COLS], f32r) for i in range(2)]
        xl = [sb(f"xl{i}", [P, COLS], f32r) for i in range(2)]
        sv = sb("sv", [SROWS, PAIRS, PC])
        sA = sb("sA", [SROWS, PAIRS, PC], f32r)
        sB = sb("sB", [SROWS, PAIRS, PC], f32r)
        msg = sb("msg", [P, PAIRS, BLK, D])
        adjT = sb("adjT", [P, GB, PAR, N])
        amat = sb("amat", [P, GB, PAR, N])
        nmph = sb("nmph", [P, COLS], f32r)
        nmpl = sb("nmpl", [P, COLS], f32r)
        h1 = sb("h1", [P, GB, PAR, TL])
        dv = sb("dv", [P, 2, GB, TL])
        sth = sb("sth", [P, 3, GB, TL], f32r)
        stl = sb("stl", [P, 3, GB, TL], f32r)
        usum = sb("usum", [P, GB, PAR, T])
        pre = sb("pre", [P, GB, PAR, T])
        xch = sb("xch", [P, GB, PAR, T], f32r)
        xcl = sb("xcl", [P, GB, PAR, T], f32r)
        tr = sb("tr", [P, PAIRS, PC])
        tz = sb("tz", [P, PAIRS, PC])
        ghn = sb("ghn", [P, PAIRS, PC])
        nn = sb("nn", [P, PAIRS, PC])
        df = sb("df", [P, PAIRS, PC])
        stats = sb("stats", [P, 2, PAIRS, BLK, 6])
        mv = sb("mv", [P, 2, PAIRS, BLK, 2])
        rstd = sb("rstd", [P, 2, PAIRS, BLK])
        xn = sb("xn", [P, PAIRS, BLK, D])
        hh = sb("hh", [P, PAIRS, PC], f32r)
        hl = sb("hl", [P, PAIRS, PC], f32r)
        tail = sb("tail", [P, (HID // P + 1) * COLS])
        hid = tail[:, 0:HID // P * COLS].rearrange("p (h f n) -> p h f n", h=PAIRS, f=HID // P)
        ot = tail[:, HID // P * COLS:].rearrange("p (h k d) -> p h k d", h=PAIRS, k=BLK)

        c2raw = tail[:, 0:P * TAPS].rearrange("p (i k) -> p i k", k=TAPS)
        c2sum = adjT[:, :, :, :].rearrange("p b r n -> p (b r n)")[:, 0:P * NM].rearrange("p (i k) -> p i k", k=NM)
        raw = amat[:, :, :, :].rearrange("p b r n -> p (b r n)").rearrange("p (s i) -> p s i", i=P)
        wraw, c1raw, msgraw = raw[:, 0:9, :], raw[:, 9, :], raw[:, 10, :]
        w1raw = raw[:, 11:13, :].rearrange("p a b -> p (a b)")

        fb = [ctx.enter_context(nc.psum_tensor(f"front{i}", [P, PC], fp32)) for i in range(2)]
        bb = [ctx.enter_context(nc.psum_tensor(f"back{i}", [P, PC], fp32)) for i in range(3)]
        cb = [ctx.enter_context(nc.psum_tensor(f"conv{i}", [P, PC], fp32)) for i in range(3)]

        count = {}

        def stage(name, per_group):
            s = sem(name)
            count[name] = (s, per_group)
            return name

        X_LOADED = stage("x_loaded", 16)
        ADJ_LOADED = stage("adj_loaded", 16)
        STORED = [stage(f"out{h}_stored", 16) for h in range(PAIRS)]
        XT_FULL = stage("xT_full", 2)
        XV_READY = stage("xv_ready", 2)
        XH_READY = stage("xh_ready", 2)
        XL_READY = stage("xl_ready", 2)
        C1_FULL = stage("conv1_full", 2)
        H1_READY = stage("h1_ready", 2)
        DV_READY = stage("h1_diff_ready", 2)
        STH_READY = stage("stream_high_ready", 3)
        STM_READY = stage("streamM_ready", 1)
        STA_READY = stage("streamA_ready", 1)
        STB_READY = stage("streamB_ready", 1)
        S_FULL = stage("se_full", 2)
        SV_READY = stage("sv_ready", 2)
        SW_READY = stage("sw_ready", 2)
        SHI_READY = stage("s_high_ready", 2)
        SLO_READY = stage("s_low_ready", 2)
        MSG_FULL = stage("msg_full", 2)
        MSUM_READY = stage("msg_sum_ready", 2)
        MSG_READY = stage("msg_ready", 2)
        ADJT_FULL = stage("adjT_full", 4)
        ADJT_READY = stage("adjT_ready", 4)
        ADJE_READY = stage("adjT_eps_ready", 4)
        DIST_FULL = stage("dist_full", 4)
        E_READY = stage("exp_ready", 4)
        A_READY = stage("a_ready", 4)
        NMP_FULL = stage("nmp_full", 2)
        NH_READY = stage("nmp_high_ready", 2)
        NL_READY = stage("nmp_low_ready", 2)
        CM_FULL = stage("convM_full", 1)
        CA_FULL = stage("convA_full", 1)
        CB_FULL = stage("convB_full", 1)
        U_READY = stage("usum_ready", 1)
        PRE_READY = stage("pre_ready", 2)
        XCH_READY = stage("xconv_high_ready", 2)
        XCL_READY = stage("xconv_low_ready", 2)
        R_FULL = stage("gate_r_full", 2)
        HN_FULL = stage("gate_hn_full", 2)
        IN_FULL = stage("gate_in_full", 2)
        Z_FULL = stage("gate_z_full", 2)
        TR_READY = stage("tr_ready", 2)
        GHN_READY = stage("ghn_ready", 2)
        T1_READY = stage("t1_ready", 2)
        T2_READY = stage("t2_ready", 2)
        N_READY = stage("n_ready", 2)
        TZ_READY = stage("tz_ready", 2)
        DF_READY = stage("df_ready", 2)
        ZD_READY = stage("zd_ready", 2)
        F_READY = stage("f_ready", 2)
        Y2_READY = stage("y2_ready", 2)
        Y_FULL = stage("y_full", 2)
        ST1_READY = stage("stats1_ready", 2)
        MV1_READY = stage("mv1_ready", 2)
        VE1_READY = stage("var_eps1_ready", 2)
        RS1_READY = stage("rstd1_ready", 2)
        XN_READY = stage("xn_ready", 2)
        XNB_READY = stage("xnb_ready", 2)
        AGG_FULL = stage("agg_full", 2)
        HH_READY = stage("h_high_ready", 2)
        HL_READY = stage("h_low_ready", 2)
        W1_FULL = stage("w1_full", 4)
        HID_READY = stage("hid_ready", 4)
        W2_FULL = stage("w2_full", 2)
        V_READY = stage("v_ready", 2)
        ST2_READY = stage("stats2_ready", 2)
        MV2_READY = stage("mv2_ready", 2)
        VE2_READY = stage("var_eps2_ready", 2)
        RS2_READY = stage("rstd2_ready", 2)
        OT_READY = stage("out_ready", 2)

        small_loaded = sem("small_loaded")
        bcast_loaded = sem("bcast_loaded")
        wraw_loaded = sem("wraw_loaded")
        c2_loaded = sem("c2_loaded")
        se_zeroed = sem("se_zeroed")
        pads_zeroed = sem("pads_zeroed")
        prep_vec_full = sem("prep_vec_full")
        prep_vec_taken = sem("prep_vec_taken")
        prep_var = sem("prep_var")
        prep_rsqrt = sem("prep_rsqrt")
        prep_dve = sem("prep_dve")
        prep_scaled = sem("prep_scaled")
        prep_full = sem("prep_full")
        prep_high = sem("prep_high")
        prep_low = sem("prep_low")

        def wait(eng, name, g, j):
            s, per = count[name]
            v = g * per + j
            if not (isinstance(v, int) and v <= 0):
                eng.wait_ge(s, v)

        def done(ins, name):
            s, per = count[name]
            ins.then_inc(s, 16 if per == 16 else 1)

        def blocks(ap):
            return ap.rearrange("p (k c) -> p k c", c=P)

        def full(ap):
            return ap.bitcast(fp32)

        def steps(eng, step, first):
            first()
            step(-1, 1, False, False, True)
            step(0, 0, False, True, True)
            step(1, 1, True, True, True)
            with eng.Fori(0, (GROUPS - 4) // 2) as i:
                step(i * 2 + 2, 0, True, True, True)
                step(i * 2 + 3, 1, True, True, True)
            step(GROUPS - 2, 0, True, True, True)
            step(GROUPS - 1, 1, True, True, False)
            step(GROUPS, 0, True, False, False)

        NSMALL = 1 + 8 + 3 + 18
        block = ctx.enter_context(nc.Block())

        @block.sync
        def _(sp):
            def first():
                sp.dma_start(cst[:, :], t["consts"]).then_inc(small_loaded, 16)
                for r, name in enumerate(("L0_gnn_bn1_g", "L0_gnn_bn1_b", "L0_gnn_bn1_m", "L0_gnn_bn1_v",
                                          "L0_gnn_bn2_g", "L0_gnn_bn2_b", "L0_gnn_bn2_m", "L0_gnn_bn2_v")):
                    sp.dma_start(vrows[r:r + 1, :], t[name].rearrange("(a n) -> a n", a=1)).then_inc(small_loaded, 16)
                sp.dma_start(c2raw[:, :, :], t["L0_gnn_conv2_w"]).then_inc(c2_loaded, 16)
                done(sp.dma_start(x_tok[:, :, :, :].rearrange("p b r d -> p b (r d)"), x_v[0, :, :, :]), X_LOADED)
                done(sp.dma_start(adj_tok[:, :, :, :].rearrange("p b r m -> p b (r m)"), adj_v[0, :, :, :]), ADJ_LOADED)

            def step(s, u, back, mid, front):
                if mid and front:
                    wait(sp, XT_FULL, s, 2)
                    done(sp.dma_start(x_tok[:, :, :, :].rearrange("p b r d -> p b (r d)"), x_v[s + 1, :, :, :]), X_LOADED)
                    wait(sp, ADJT_FULL, s, 4)
                    done(sp.dma_start(adj_tok[:, :, :, :].rearrange("p b r m -> p b (r m)"), adj_v[s + 1, :, :, :]), ADJ_LOADED)
                if back:
                    for h in range(PAIRS):
                        wait(sp, OT_READY, s - 1, h + 1)
                        done(sp.dma_start(out_v[s - 1, h, :, :, :],
                                          ot[:, h, :, :].rearrange("p (b r) d -> p b (r d)", r=PAR)), STORED[h])

            steps(sp, step, first)
            for h in range(PAIRS):
                wait(sp, STORED[h], GROUPS - 1, 16)

        @block.gpsimd
        def _(pool):
            def first():
                pool.memset(serows[:, :], 0.0).then_inc(se_zeroed, 1)
                pool.memset(minus_half[:, :], -0.5).then_inc(pads_zeroed, 1)
                pool.memset(epst[:, 0, :], 4 * EPS).then_inc(pads_zeroed, 1)
                pool.memset(epst[:, 1, :], EPS).then_inc(pads_zeroed, 1)
                pool.memset(h1[:, :, :, :], 0.0).then_inc(pads_zeroed, 1)
                pool.memset(dv[:, :, :, :], 0.0).then_inc(pads_zeroed, 1)
                pool.dma_start(epscol[:, :], t["L1_gnn_eps"].partition_broadcast(P)).then_inc(bcast_loaded, 16)
                pool.dma_start(bmsg[:, :], t["L0_gnn_b_msg"].partition_broadcast(P)).then_inc(bcast_loaded, 16)
                pool.dma_start(b2bc[:, :], t["L1_gnn_b2"].partition_broadcast(P)).then_inc(bcast_loaded, 16)
                pool.wait_ge(bcast_loaded, 3 * 16)
                pool.wait_ge(pads_zeroed, 1)
                for k in range(2):
                    pool.wait_ge(prep_var, k + 1)
                    pool.tensor_tensor(bn[:, 4 * k:4 * k + 1], bn[:, 4 * k + 3:4 * k + 4],
                                       minus_half[:, 0:1], ALU.pow).then_inc(prep_rsqrt, 1)

            def differences(g):
                wait(pool, H1_READY, g, 2)
                if not isinstance(g, int) or g > 0:
                    wait(pool, STA_READY, g - 1, 1)
                else:
                    pool.wait_ge(pads_zeroed, 5)
                done(pool.tensor_tensor(dv[:, 0, :, :], h1[:, :, 0, :], h1[:, :, 1, :], ALU.subtract), DV_READY)
                wait(pool, STB_READY, g - 1, 1)
                done(pool.tensor_tensor(dv[:, 1, :, 0:TL - 1], h1[:, :, 0, 1:TL], h1[:, :, 1, 0:TL - 1],
                                        ALU.subtract), DV_READY)

            def rsqrt(k, g, h, mv_ready, ve_ready, rs_ready):
                wait(pool, mv_ready, g, h + 1)
                done(pool.tensor_tensor(rstd[:, k, h, :], mv[:, k, h, :, 1], epst[:, k, :], ALU.add), ve_ready)
                wait(pool, ve_ready, g, h + 1)
                done(pool.tensor_tensor(rstd[:, k, h, :], rstd[:, k, h, :], minus_half[:, :], ALU.pow), rs_ready)

            def step(s, u, back, mid, front):
                gb, gm, gf = s - 1, s, s + 1
                if back:
                    for h in range(PAIRS):
                        c = slice(h * PC, (h + 1) * PC)
                        wait(pool, N_READY, gb, h + 1)
                        done(pool.tensor_tensor(df[:, h, :], xv[1 - u][:, c], nn[:, h, :], ALU.subtract), DF_READY)
                        wait(pool, TZ_READY, gb, h + 1)
                        wait(pool, DF_READY, gb, h + 1)
                        done(pool.tensor_tensor(df[:, h, :], tz[:, h, :], df[:, h, :], ALU.mult), ZD_READY)
                    for h in range(PAIRS):
                        rsqrt(0, gb, h, MV1_READY, VE1_READY, RS1_READY)
                    for h in range(PAIRS):
                        wait(pool, XN_READY, gb, h + 1)
                        wait(pool, STORED[h], gb - 1, 16)
                        done(pool.tensor_tensor(ot[:, h, :, :], xn[:, h, :, :],
                                                b2bc[:, :].unsqueeze(1).to_broadcast([P, BLK, D]), ALU.add), XNB_READY)
                if mid:
                    for b in range(GB):
                        if b == 2 and back:
                            rsqrt(1, gb, 0, MV2_READY, VE2_READY, RS2_READY)
                        wait(pool, ADJT_READY, gm, b + 1)
                        wait(pool, E_READY, gm, b + 1)
                        done(pool.tensor_tensor(amat[:, b, :, :], amat[:, b, :, :], adjT[:, b, :, :], ALU.mult), A_READY)
                    for b in range(GB):
                        a = adjT[:, b, :, :].rearrange("p r n -> p (r n)")
                        dg = bass.AP(a.tensor, a.offset, [a.ap[0], [N + P, PAR], [1, P]])
                        wait(pool, A_READY, gm, b + 1)
                        done(pool.tensor_tensor(dg, dg, diag[:, :].unsqueeze(1).to_broadcast([P, PAR, P]), ALU.add),
                             ADJE_READY)
                if back:
                    if not mid:
                        rsqrt(1, gb, 0, MV2_READY, VE2_READY, RS2_READY)
                    rsqrt(1, gb, 1, MV2_READY, VE2_READY, RS2_READY)
                if front:
                    differences(gf)

            steps(pool, step, first)

        @block.scalar
        def _(act):
            def first():
                for r, name, rows in ((BIH, "L0_gnn_b_ih", 3), (BHH, "L0_gnn_b_hh", 3), (B1, "L1_gnn_b1", 2)):
                    act.dma_start(vrows[r:r + rows, :], t[name].rearrange("(a n) -> a n", a=rows)).then_inc(small_loaded, 16)
                act.dma_start(c1raw, t["L0_gnn_conv1_w"].rearrange("o i k -> o (i k)")).then_inc(wraw_loaded, 16)
                act.wait_ge(se_zeroed, 1)
                for q in range(3):
                    for j in range(3):
                        r = 32 * q + NSE * j
                        act.dma_start(serows[r:r + NSE, 0:P], t["L0_gnn_w_se"]).then_inc(small_loaded, 16)
                        act.dma_start(serows[r:r + NSE, P:P + 1],
                                      t["L0_gnn_b_se"].rearrange("(a n) -> a n", n=1)).then_inc(small_loaded, 16)
                act.dma_start(msgraw, t["L0_gnn_w_msg"]).then_inc(wraw_loaded, 16)
                act.dma_start(wraw[:, 0:6, :].rearrange("p (g s) i -> p g (s i)", g=3),
                              t["L0_gnn_w_ih"].rearrange("(g o) i -> o g i", g=3)).then_inc(wraw_loaded, 16)
                act.dma_start(wraw[:, 6:9, :], t["L0_gnn_w_hh"].rearrange("(g o) i -> o g i", g=3)).then_inc(wraw_loaded, 16)
                act.dma_start(w1raw, t["L1_gnn_W1"]).then_inc(wraw_loaded, 16)
                act.dma_start(w2[:, :, :], t["L1_gnn_W2"].rearrange("(f p) d -> p f d", p=P)).then_inc(wraw_loaded, 16)
                act.wait_ge(prep_vec_full, 1)
                act.activation(vec[:, :], fb[0][:, 0:NVEC], ACT.Copy).then_inc(prep_vec_taken, 1)
                act.activation(wmsgT[:, :], fb[0][:, 256:256 + P], ACT.Copy).then_inc(prep_vec_taken, 1)
                act.activation(wseh[:, :], fb[0][:, 128:128 + SROWS], ACT.Copy).then_inc(prep_vec_taken, 1)
                act.activation(w1h[:, :], w1raw, ACT.Copy).then_inc(prep_vec_taken, 1)
                for k in range(NSLOT // SB):
                    act.wait_ge(prep_full, k + 1)
                    act.activation(wh[:, SB * k:SB * (k + 1), :], blocks(fb[(k + 1) % 2][:, :]), ACT.Copy).then_inc(prep_high, 1)

            def step(s, u, back, mid, front):
                gb, gm, gf = s - 1, s, s + 1
                if mid:
                    for h in range(PAIRS):
                        wait(act, S_FULL, gm, h + 1)
                        done(act.activation(sv[:, h, :], fb[h][0:SROWS, :], ACT.Identity,
                                            bias=sescale[:, 0:1], scale=cst[0:SROWS, P + SQ_MASK:P + SQ_MASK + 1]), SV_READY)
                    for h in range(PAIRS):
                        wait(act, SW_READY, gm, h + 1)
                        act.activation(sA[:, h, :], sv[:, h, :], ACT.Identity,
                                       bias=cst[0:SROWS, P + A_ADD:P + A_ADD + 1], scale=cst[0:SROWS, P + A_MUL:P + A_MUL + 1])
                        done(act.activation(sB[:, h, :], sv[:, h, :], ACT.Identity,
                                            bias=cst[0:SROWS, P + B_ADD:P + B_ADD + 1],
                                            scale=cst[0:SROWS, P + B_MUL:P + B_MUL + 1]), SHI_READY)
                if back:
                    for h in range(PAIRS):
                        r_bank, hn_bank, _, z_bank = (bb[(4 * h + k) % 3] for k in range(4))
                        wait(act, R_FULL, gb, h + 1)
                        done(act.activation(tr[:, h, :], r_bank[:, :], ACT.Tanh, bias=gbias[:, 0:1], scale=0.5), TR_READY)
                        wait(act, HN_FULL, gb, h + 1)
                        done(act.activation(ghn[:, h, :], hn_bank[:, :], ACT.Identity, bias=gbias[:, 2:3], scale=0.5), GHN_READY)
                        wait(act, T2_READY, gb, h + 1)
                        done(act.activation(nn[:, h, :], ghn[:, h, :], ACT.Tanh, bias=gbias[:, 3:4]), N_READY)
                        wait(act, Z_FULL, gb, h + 1)
                        done(act.activation(tz[:, h, :], z_bank[:, :], ACT.Tanh, bias=gbias[:, 1:2], scale=0.5), TZ_READY)
                if mid:
                    xconv_high(gm, 0)
                if back:
                    for h in range(PAIRS):
                        wait(act, AGG_FULL, gb, h + 1)
                        done(act.activation(hh[:, h, :], bb[(10 + h) % 3][:, :], ACT.Copy), HH_READY)
                if mid:
                    adj_out(gm, 0)
                if back:
                    hidden(gb, 0)
                if mid:
                    adj_out(gm, 1)
                    exps(gm, 0)
                if back:
                    hidden(gb, 1)
                if mid:
                    exps(gm, 1)
                    for h in range(PAIRS):
                        wait(act, NMP_FULL, gm, h + 1)
                        done(act.activation(nmph[:, h * PC:(h + 1) * PC], fb[h][:, :], ACT.Copy), NH_READY)
                if front:
                    for h in range(PAIRS):
                        c = slice(h * PC, (h + 1) * PC)
                        wait(act, XT_FULL, gf, h + 1)
                        done(act.activation(xv[1 - u][:, c], fb[h][:, :], ACT.Copy), XV_READY)
                        done(act.activation(xh[1 - u][:, c], fb[h][:, :], ACT.Copy), XH_READY)
                    if isinstance(gf, int) and gf == 0:
                        act.wait_ge(pads_zeroed, 5)
                    else:
                        wait(act, DV_READY, gf - 1, 2)
                        wait(act, STM_READY, gf - 1, 1)
                    for h in range(PAIRS):
                        wait(act, C1_FULL, gf, h + 1)
                        done(act.activation(
                            h1[:, 2 * h:2 * h + 2, :, PAD:PAD + T].rearrange("p b r t -> p (b r) t"),
                            blocks(fb[h][:, :]), ACT.Relu, bias=bn[:, 3:4]), H1_READY)
                if mid:
                    xconv_high(gm, 1)

            def xconv_high(g, par):
                wait(act, PRE_READY, g, par + 1)
                done(act.activation(xch[:, :, par, :], pre[:, :, par, :], ACT.Relu), XCH_READY)

            def adj_out(g, h):
                for b in (2 * h, 2 * h + 1):
                    wait(act, ADJT_FULL, g, b + 1)
                    done(act.activation(adjT[:, b, :, :].rearrange("p r n -> p (r n)"), fb[b % 2][:, :], ACT.Copy), ADJT_READY)

            def exps(g, h):
                for b in (2 * h, 2 * h + 1):
                    wait(act, DIST_FULL, g, b + 1)
                    done(act.activation(amat[:, b, :, :].rearrange("p r n -> p (r n)"), fb[b % 2][:, :], ACT.Exp), E_READY)

            def hidden(g, h):
                for f in range(2):
                    wait(act, W1_FULL, g, 2 * h + f + 1)
                    done(act.activation(hid[:, h, f, :], bb[(12 + 2 * h + f) % 3][:, :], ACT.Relu,
                                        bias=vec[:, B1 + f:B1 + f + 1]), HID_READY)

            steps(act, step, first)

        @block.vector
        def _(dve):
            def first():
                n = [0]

                def link(ins):
                    n[0] += 1
                    ins.then_inc(prep_dve, 1)
                    dve.wait_ge(prep_dve, n[0])

                dve.wait_ge(prep_vec_taken, 4)
                dve.wait_ge(bcast_loaded, 3 * 16)
                link(dve.tensor_tensor(wsel[:, :], fb[0][:, 128:128 + SROWS], full(wseh[:, :]), ALU.subtract))
                link(dve.tensor_tensor(w1l[:, :], w1raw, full(w1h[:, :]), ALU.subtract))
                for k in range(2):
                    dve.tensor_scalar(bn[:, 4 * k + 3:4 * k + 4], vec[:, 4 * k + 3:4 * k + 4], EPS, None,
                                      ALU.add).then_inc(prep_var, 1)
                link(dve.scalar_tensor_tensor(diag[:, :], ident, epscol[:, 0:1], ident, ALU.mult, ALU.add))
                link(dve.scalar_tensor_tensor(sescale[:, :], serows[:, P:P + 1], cst[0:SROWS, P + SQ_MASK:P + SQ_MASK + 1],
                                              cst[0:SROWS, P + LIN_ONE:P + LIN_ONE + 1], ALU.mult, ALU.add))
                link(dve.tensor_tensor(gbias[:, 0:3], vec[:, BIH:BIH + 3], vec[:, BHH:BHH + 3], ALU.add))
                link(dve.tensor_scalar(gbias[:, 0:2], gbias[:, 0:2], 0.5, None, ALU.mult))
                link(dve.tensor_scalar(gbias[:, 2:3], vec[:, BHH + 2:BHH + 3], 0.5, None, ALU.mult))
                link(dve.tensor_copy(gbias[:, 3:4], vec[:, BIH + 2:BIH + 3]))
                dve.wait_ge(prep_rsqrt, 2)
                for k in range(2):
                    c = 4 * k
                    link(dve.tensor_tensor(bn[:, c + 1:c + 2], bn[:, c:c + 1], vec[:, c:c + 1], ALU.mult))
                    link(dve.tensor_tensor(bn[:, c + 2:c + 3], bn[:, c + 1:c + 2], vec[:, c + 2:c + 3], ALU.mult))
                    link(dve.tensor_tensor(bn[:, c + 3:c + 4], vec[:, c + 1:c + 2], bn[:, c + 2:c + 3], ALU.subtract))
                dve.wait_ge(wraw_loaded, 6 * 16)
                dve.tensor_scalar(c1raw, c1raw, bn[:, 1:2], None, ALU.mult).then_inc(prep_scaled, 1)
                dve.wait_ge(c2_loaded, 16)
                link(dve.tensor_scalar(c2raw[:, :, :], c2raw[:, :, :], bn[:, 5:6], None, ALU.mult))
                dve.tensor_copy(c2sum[:, :, NM - 1], c2raw[:, :, TAPS - 1]).then_inc(prep_scaled, 1)
                dve.tensor_tensor(c2sum[:, :, 0:NM - 1], c2raw[:, :, 0:TAPS - 1:2], c2raw[:, :, 1:TAPS:2],
                                  ALU.add).then_inc(prep_scaled, 1)
                for k in range(NSLOT // SB):
                    dve.wait_ge(prep_high, k + 1)
                    dve.tensor_tensor(wl[:, SB * k:SB * (k + 1), :], blocks(fb[(k + 1) % 2][:, :]),
                                      full(wh[:, SB * k:SB * (k + 1), :]), ALU.subtract).then_inc(prep_low, 1)

            def split(g, st, src, wait_for, ready):
                done(dve.tensor_copy(sth[:, st, :, :], src), STH_READY)
                wait(dve, STH_READY, g, st + 1)
                done(dve.tensor_tensor(stl[:, st, :, :], src, full(sth[:, st, :, :]), ALU.subtract), ready)

            def pre_sum(g, par):
                wait(dve, (CA_FULL, CB_FULL)[par], g, 1)
                wait(dve, U_READY, g, 1)
                done(dve.scalar_tensor_tensor(pre[:, :, par, :], cb[1 + par][:, :].rearrange("p (b t) -> p b t", t=T),
                                              bn[:, 7:8], usum[:, :, par, :], ALU.add, ALU.add), PRE_READY)

            def xconv_low(g, par):
                wait(dve, XCH_READY, g, par + 1)
                done(dve.scalar_tensor_tensor(xcl[:, :, par, :], pre[:, :, par, :], 0.0, full(xch[:, :, par, :]),
                                              ALU.max, ALU.subtract), XCL_READY)

            def norm_stats(k, g, h, src, st_ready, mv_ready):
                for q in range(BLK):
                    last = dve.bn_stats(stats[:, k, h, q, :], src(q))
                done(last, st_ready)
                wait(dve, st_ready, g, h + 1)
                dve.nop(nofuse=True)
                for q in range(BLK):
                    last = dve.bn_aggr(mv[:, k, h, q, :], stats[:, k, h, q, :])
                done(last, mv_ready)

            def norm_apply(k, g, h, src, dst, rs_ready, ready):
                wait(dve, rs_ready, g, h + 1)
                for q in range(BLK):
                    last = dve.tensor_scalar(dst(q), src(q), mv[:, k, h, q, 0:1], rstd[:, k, h, q:q + 1],
                                             ALU.subtract, ALU.mult)
                done(last, ready)

            def second_norm(g, h):
                wait(dve, W2_FULL, g, h + 1)
                wait(dve, XNB_READY, g, h + 1)
                done(dve.tensor_tensor(ot[:, h, :, :].rearrange("p k d -> p (k d)"), bb[(16 + h) % 3][:, :],
                                       ot[:, h, :, :].rearrange("p k d -> p (k d)"), ALU.add), V_READY)
                wait(dve, V_READY, g, h + 1)
                norm_stats(1, g, h, lambda q: ot[:, h, q, :], ST2_READY, MV2_READY)

            def second_apply(g, h):
                norm_apply(1, g, h, lambda q: ot[:, h, q, :], lambda q: ot[:, h, q, :], RS2_READY, OT_READY)

            def step(s, u, back, mid, front):
                gb, gm, gf = s - 1, s, s + 1
                if mid:
                    for h in range(PAIRS):
                        wait(dve, SV_READY, gm, h + 1)
                        done(dve.scalar_tensor_tensor(sv[:, h, :], fb[h][0:SROWS, :], serows[:, P:P + 1], sv[:, h, :],
                                                      ALU.add, ALU.mult), SW_READY)
                    for h in range(PAIRS):
                        wait(dve, MSG_FULL, gm, h + 1)
                        done(dve.tensor_tensor(msg[:, h, :, :], blocks(fb[h][:, :]),
                                               bmsg[:, :].unsqueeze(1).to_broadcast([P, BLK, D]), ALU.add), MSUM_READY)
                        wait(dve, MSUM_READY, gm, h + 1)
                        done(dve.tensor_scalar(msg[:, h, :, :], msg[:, h, :, :], 0.0, None, ALU.max), MSG_READY)
                    for h in range(PAIRS):
                        wait(dve, SHI_READY, gm, h + 1)
                        dve.scalar_tensor_tensor(sA[0:32, h, :], sv[0:32, h, :], cst[0:32, P + A_MUL:P + A_MUL + 1],
                                                 full(sA[0:32, h, :]), ALU.mult, ALU.subtract)
                        done(dve.scalar_tensor_tensor(sB[64:96, h, :], sv[64:96, h, :], cst[64:96, P + B_MUL:P + B_MUL + 1],
                                                      full(sB[64:96, h, :]), ALU.mult, ALU.subtract), SLO_READY)
                    wait(dve, CM_FULL, gm, 1)
                    done(dve.tensor_tensor(usum[:, :, :, :],
                                           cb[0][:, :].rearrange("p (b t) -> p b t", t=T).unsqueeze(2).to_broadcast([P, GB, PAR, T]),
                                           xv[u][:, :].rearrange("p (b r t) -> p b r t", b=GB, r=PAR), ALU.add), U_READY)
                if back:
                    for h in range(PAIRS):
                        c = slice(h * PC, (h + 1) * PC)
                        wait(dve, GHN_READY, gb, h + 1)
                        wait(dve, TR_READY, gb, h + 1)
                        done(dve.scalar_tensor_tensor(ghn[:, h, :], tr[:, h, :], 1.0, ghn[:, h, :], ALU.add, ALU.mult), T1_READY)
                        wait(dve, IN_FULL, gb, h + 1)
                        wait(dve, T1_READY, gb, h + 1)
                        done(dve.tensor_tensor(ghn[:, h, :], bb[(4 * h + 2) % 3][:, :], ghn[:, h, :], ALU.add), T2_READY)
                        wait(dve, N_READY, gb, h + 1)
                        done(dve.scalar_tensor_tensor(tr[:, h, :], xv[1 - u][:, c], 3.0, nn[:, h, :], ALU.mult, ALU.add), F_READY)
                        wait(dve, ZD_READY, gb, h + 1)
                        wait(dve, F_READY, gb, h + 1)
                        done(dve.tensor_tensor(tr[:, h, :], tr[:, h, :], df[:, h, :], ALU.add), Y2_READY)
                    for h in range(PAIRS):
                        bank = bb[(8 + h) % 3]
                        wait(dve, Y_FULL, gb, h + 1)
                        norm_stats(0, gb, h, lambda q: bank[:, q * P:(q + 1) * P], ST1_READY, MV1_READY)
                        norm_apply(0, gb, h, lambda q: bank[:, q * P:(q + 1) * P], lambda q: xn[:, h, q, :], RS1_READY, XN_READY)
                if mid:
                    pre_sum(gm, 0)
                if back:
                    for h in range(PAIRS):
                        wait(dve, HH_READY, gb, h + 1)
                        done(dve.tensor_tensor(hl[:, h, :], bb[(10 + h) % 3][:, :], full(hh[:, h, :]), ALU.subtract), HL_READY)
                if mid:
                    xconv_low(gm, 0)
                if back:
                    second_norm(gb, 0)
                    second_apply(gb, 0)
                if mid:
                    nmp_low(gm, 0)
                if back:
                    second_norm(gb, 1)
                if mid:
                    nmp_low(gm, 1)
                if back:
                    second_apply(gb, 1)
                if front:
                    for h in range(PAIRS):
                        c = slice(h * PC, (h + 1) * PC)
                        wait(dve, XH_READY, gf, h + 1)
                        done(dve.tensor_tensor(xl[1 - u][:, c], fb[h][:, :], full(xh[1 - u][:, c]), ALU.subtract), XL_READY)
                    wait(dve, H1_READY, gf, 2)
                    wait(dve, CM_FULL, gf - 1, 1)
                    split(gf, 0, h1[:, :, 1, :], None, STM_READY)
                if mid:
                    pre_sum(gm, 1)
                if front:
                    wait(dve, DV_READY, gf, 2)
                    wait(dve, CA_FULL, gf - 1, 1)
                    split(gf, 1, dv[:, 0, :, :], None, STA_READY)
                if mid:
                    xconv_low(gm, 1)
                if front:
                    wait(dve, CB_FULL, gf - 1, 1)
                    split(gf, 2, dv[:, 1, :, :], None, STB_READY)

            def nmp_low(g, h):
                c = slice(h * PC, (h + 1) * PC)
                wait(dve, NH_READY, g, h + 1)
                done(dve.tensor_tensor(nmpl[:, c], fb[h][:, :], full(nmph[:, c]), ALU.subtract), NL_READY)

            steps(dve, step, first)

        @block.tensor
        def _(pe):
            def products(bank, terms, first=True, last=True):
                todo = [(a, b) for (ah, al, bh, bl) in terms for (a, b) in ((ah, bh), (ah, bl), (al, bh))]
                for k, (a, b) in enumerate(todo):
                    ins = pe.matmul(bank, a, b, start=first and k == 0, stop=last and k == len(todo) - 1)
                return ins

            def first():
                pe.wait_ge(small_loaded, NSMALL * 16)
                pe.wait_ge(wraw_loaded, 6 * 16)
                pe.transpose(fb[0][:, 0:NVEC], vrows[:, :], cst[0:NVEC, 0:NVEC])
                pe.transpose(fb[0][:, 128:128 + SROWS], serows[:, 0:P], cst[0:SROWS, 0:SROWS])
                pe.transpose(fb[0][:, 256:256 + P], msgraw, ident).then_inc(prep_vec_full, 1)
                src = {("conv1", 0): c1raw}
                for k in range(NM):
                    src[("M", k)] = c2sum[:, :, k]
                    src[("A", k)] = c2raw[:, :, 2 * k]
                for k in range(NR):
                    src[("B", k)] = c2raw[:, :, 2 * k + 1]
                for g in range(3):
                    src[("conv", g)] = wraw[:, 2 * g, :]
                    src[("nmp", g)] = wraw[:, 2 * g + 1, :]
                    src[("hid", g)] = wraw[:, 6 + g, :]
                pe.wait_ge(prep_scaled, 3)
                for n, key in enumerate(SLOT):
                    k = n // SB
                    if n % SB == 0 and k >= 2:
                        pe.wait_ge(prep_low, k - 1)
                    ins = pe.transpose(fb[(k + 1) % 2][:, (n % SB) * P:(n % SB + 1) * P], src[key], ident)
                    if n % SB == SB - 1:
                        ins.then_inc(prep_full, 1)

            def wslot(name, k):
                i = SLOT[(name, k)]
                return wh[:, i, :], wl[:, i, :]

            def taps(g, which, k0, k1):
                st = "MAB".index(which)
                n = (NM, NP_, NR)[st]
                if k0 == 0:
                    wait(pe, (STM_READY, STA_READY, STB_READY)[st], g, 1)
                    if st == 0:
                        wait(pe, U_READY, g - 1, 1)
                    else:
                        wait(pe, PRE_READY, g - 1, st)
                bank = cb[st][:, :].rearrange("p (b t) -> p b t", t=T)
                for k in range(k0, k1):
                    ins = products(bank, [wslot(which, k) + (sth[:, st, :, k:k + T], stl[:, st, :, k:k + T])],
                                   first=k == 0, last=k == n - 1)
                if k1 == n:
                    done(ins, (CM_FULL, CA_FULL, CB_FULL)[st])

            def x_transpose(g, h):
                if h == 0:
                    wait(pe, X_LOADED, g, 16)
                wait(pe, NL_READY, g - 1, h + 1)
                if isinstance(g, int) and g == 0 and h == 0:
                    pe.wait_ge(prep_low, NSLOT // SB)
                for q in range(BLK):
                    ins = pe.transpose(fb[h][:, q * P:(q + 1) * P], x_tok[:, 2 * h + q // 2, q % 2, :], ident)
                done(ins, XT_FULL)

            def conv1(g, u, h):
                c = slice(h * PC, (h + 1) * PC)
                wait(pe, XL_READY, g, h + 1)
                done(products(fb[h][:, :], [wslot("conv1", 0) + (xh[u][:, c], xl[u][:, c])]), C1_FULL)

            def embed(g, u, h):
                c = slice(h * PC, (h + 1) * PC)
                wait(pe, H1_READY, g, h + 1)
                done(products(fb[h][0:SROWS, :], [(wseh[:, :], wsel[:, :], xh[u][:, c], xl[u][:, c])]), S_FULL)

            def messages(g, u, h):
                wait(pe, SW_READY, g, h + 1)
                for q in range(BLK):
                    ins = pe.matmul(fb[h][:, q * P:(q + 1) * P], xv[u][:, h * PC + q * P:h * PC + (q + 1) * P], wmsgT[:, :],
                                    start=True, stop=True)
                done(ins, MSG_FULL)

            def adj_transpose(g, b):
                if b == 0:
                    wait(pe, ADJ_LOADED, g, 16)
                if b < 2:
                    wait(pe, MSUM_READY, g, b + 1)
                else:
                    wait(pe, ADJT_READY, g, b - 1)
                for rm in range(PAR):
                    for rn in range(PAR):
                        ins = pe.transpose(fb[b % 2][:, rm * N + rn * P:rm * N + (rn + 1) * P],
                                           adj_tok[:, b, rn, rm:N:PAR], ident)
                done(ins, ADJT_FULL)

            def distances(g, b):
                if b < 2:
                    wait(pe, ADJT_READY, g, b + 3)
                else:
                    wait(pe, E_READY, g, b - 1)
                wait(pe, SLO_READY, g, b // 2 + 1)
                h, o = b // 2, (b % 2) * N
                for rm in range(PAR):
                    ins = pe.matmul(fb[b % 2][:, rm * N:(rm + 1) * N], sA[:, h, o + rm * P:o + (rm + 1) * P],
                                    sB[:, h, o:o + N], start=True, stop=True)
                done(ins, DIST_FULL)

            def gather(bank, lhs, rhs):
                for b in range(2):
                    for rm in range(PAR):
                        ins = pe.matmul(bank[:, b * N:(b + 1) * N], lhs(b, rm), rhs(b, rm), start=rm == 0, stop=rm == PAR - 1)
                return ins

            def nmp(g, h):
                wait(pe, E_READY, g, h + 3)
                wait(pe, MSG_READY, g, h + 1)
                wait(pe, A_READY, g, 2 * h + 2)
                done(gather(fb[h], lambda b, rm: msg[:, h, 2 * b + rm, :], lambda b, rm: amat[:, 2 * h + b, rm, :]), NMP_FULL)

            def gates(g, u, h):
                c = slice(h * PC, (h + 1) * PC)
                xx = (xh[u][:, c], xl[u][:, c])
                nm = (nmph[:, c], nmpl[:, c])
                xc = (xch[:, 2 * h:2 * h + 2, :, :].rearrange("p b r t -> p (b r t)"),
                      xcl[:, 2 * h:2 * h + 2, :, :].rearrange("p b r t -> p (b r t)"))
                r_bank, hn_bank, in_bank, z_bank = (bb[(4 * h + k) % 3][:, :] for k in range(4))
                if h == 0:
                    wait(pe, HID_READY, g - 1, 4)
                    wait(pe, NL_READY, g, 2)
                    wait(pe, XCL_READY, g, 2)
                else:
                    wait(pe, GHN_READY, g, 1)
                done(products(r_bank, [wslot("hid", 0) + xx, wslot("nmp", 0) + nm, wslot("conv", 0) + xc]), R_FULL)
                if h == 0:
                    wait(pe, V_READY, g - 1, 2)
                else:
                    wait(pe, T2_READY, g, 1)
                done(products(hn_bank, [wslot("hid", 2) + xx]), HN_FULL)
                if h == 1:
                    wait(pe, TZ_READY, g, 1)
                done(products(in_bank, [wslot("nmp", 2) + nm, wslot("conv", 2) + xc]), IN_FULL)
                wait(pe, TR_READY, g, h + 1)
                done(products(z_bank, [wslot("hid", 1) + xx, wslot("nmp", 1) + nm, wslot("conv", 1) + xc]), Z_FULL)

            def y_transpose(g, h):
                wait(pe, (GHN_READY, T2_READY)[h], g, 2)
                wait(pe, Y2_READY, g, h + 1)
                for q in range(BLK):
                    ins = pe.transpose(bb[(8 + h) % 3][:, q * P:(q + 1) * P], tr[:, h, q * P:(q + 1) * P], ident)
                done(ins, Y_FULL)

            def aggregate(g, h):
                if h == 0:
                    wait(pe, TZ_READY, g, 2)
                wait(pe, XN_READY, g, h + 1)
                wait(pe, ADJE_READY, g, 2 * h + 2)
                done(gather(bb[(10 + h) % 3], lambda b, rm: xn[:, h, 2 * b + rm, :], lambda b, rm: adjT[:, 2 * h + b, rm, :]),
                     AGG_FULL)

            def mlp1(g, h):
                for f in range(2):
                    if h == 0:
                        wait(pe, (XN_READY, HL_READY)[f], g, 2 - f)
                        if f == 0:
                            wait(pe, HL_READY, g, 1)
                    else:
                        wait(pe, (HL_READY, HID_READY)[f], g, 2 - f)
                    done(products(bb[(12 + 2 * h + f) % 3][:, :],
                                  [(w1h[:, f * P:(f + 1) * P], w1l[:, f * P:(f + 1) * P], hh[:, h, :], hl[:, h, :])]), W1_FULL)

            def mlp2(g, h):
                wait(pe, HID_READY, g, 2 * h + 2)
                if h == 1:
                    wait(pe, HID_READY, g, 4)
                for q in range(BLK):
                    for f in range(2):
                        ins = pe.matmul(bb[(16 + h) % 3][:, q * P:(q + 1) * P], hid[:, h, f, q * P:(q + 1) * P], w2[:, f, :],
                                        start=f == 0, stop=f == 1)
                done(ins, W2_FULL)

            def step(s, u, back, mid, front):
                gb, gm, gf, ub = s - 1, s, s + 1, 1 - u
                if mid:
                    taps(gm, "M", 0, 4)
                    embed(gm, u, 0)
                    embed(gm, u, 1)
                    taps(gm, "M", 4, 6)
                    messages(gm, u, 0)
                    messages(gm, u, 1)
                    taps(gm, "M", 6, NM)
                if back:
                    gates(gb, ub, 0)
                    gates(gb, ub, 1)
                    y_transpose(gb, 0)
                if mid:
                    taps(gm, "A", 0, 4)
                if back:
                    y_transpose(gb, 1)
                if mid:
                    taps(gm, "A", 4, NP_)
                if back:
                    aggregate(gb, 0)
                    aggregate(gb, 1)
                if mid:
                    adj_transpose(gm, 0)
                    adj_transpose(gm, 1)
                if back:
                    mlp1(gb, 0)
                if mid:
                    adj_transpose(gm, 2)
                    adj_transpose(gm, 3)
                    distances(gm, 0)
                    distances(gm, 1)
                    taps(gm, "B", 0, 1)
                if back:
                    mlp1(gb, 1)
                    mlp2(gb, 0)
                if mid:
                    distances(gm, 2)
                    distances(gm, 3)
                    taps(gm, "B", 1, 3)
                    nmp(gm, 0)
                if back:
                    mlp2(gb, 1)
                if mid:
                    nmp(gm, 1)
                if front:
                    x_transpose(gf, 0)
                    x_transpose(gf, 1)
                if mid:
                    taps(gm, "B", 3, 5)
                if front:
                    conv1(gf, ub, 0)
                    conv1(gf, ub, 1)
                if mid:
                    taps(gm, "B", 5, NR)

            steps(pe, step, first)


_INS = ['x', 'adj', 'L0_gnn_w_se', 'L0_gnn_b_se', 'L0_gnn_conv1_w', 'L0_gnn_bn1_g', 'L0_gnn_bn1_b', 'L0_gnn_bn1_m',
        'L0_gnn_bn1_v', 'L0_gnn_conv2_w', 'L0_gnn_bn2_g', 'L0_gnn_bn2_b', 'L0_gnn_bn2_m', 'L0_gnn_bn2_v', 'L0_gnn_w_msg',
        'L0_gnn_b_msg', 'L0_gnn_w_ih', 'L0_gnn_b_ih', 'L0_gnn_w_hh', 'L0_gnn_b_hh', 'L1_gnn_eps', 'L1_gnn_W1', 'L1_gnn_b1',
        'L1_gnn_W2', 'L1_gnn_b2']


def kernel(**inputs):
    import numpy as _np
    import concourse.bacc as _bacc
    from concourse import mybir as _mybir
    from concourse.bass_utils import run_bass_kernel_spmd as _run

    nc = _bacc.Bacc("TRN2", target_bir_lowering=False, num_devices=1)
    arrays, aps = {}, {}
    for name in _INS:
        a = _np.ascontiguousarray(inputs[name])
        arrays[f"in_{name}_dram"] = a
        aps[name] = nc.dram_tensor(f"in_{name}_dram", a.shape, _mybir.dt.from_np(a.dtype), kind="ExternalInput").ap()
    c = shape_constants()
    arrays["in_consts_dram"] = c
    aps["consts"] = nc.dram_tensor("in_consts_dram", c.shape, _mybir.dt.from_np(c.dtype), kind="ExternalInput").ap()
    out = nc.dram_tensor("out_0_dram", (B, N, D), _mybir.dt.float32, kind="ExternalOutput").ap()
    gnn_kernel(nc, aps, out)
    r = _run(nc, [arrays], core_ids=[0])
    return r.results[0]["out_0_dram"]
```

```python
import concourse.bass as bass
from concourse import mybir
from contextlib import ExitStack
import numpy as np

B, N, D = 32, 256, 128
TAPS = 17
HID = 256
NSE = 3
EPS = 1e-5

GB = 4
GROUPS = B // GB
P = 128
PAR = N // P
T = N // PAR
PAIRS = GB // 2
COLS = GB * N
PC = COLS // PAIRS
BLK = PC // P
PAD = (TAPS // 2) // PAR
TL = T + 2 * PAD
NM, NP_, NR = (TAPS + 1) // 2, (TAPS + 1) // 2, TAPS // 2

SLOT = {("conv1", 0): 0}
for _name, _n in (("M", NM), ("A", NP_), ("B", NR), ("hid", 3), ("nmp", 3), ("conv", 3)):
    for _k in range(_n):
        SLOT[(_name, _k)] = len(SLOT)
NSLOT = len(SLOT)
S_M, S_A, S_B, S_GATE = (SLOT[(n, 0)] for n in ("M", "A", "B", "hid"))

(BN1_G, BN1_B, BN1_M, BN1_V, BN2_G, BN2_B, BN2_M, BN2_V,
 BIH, BHH, B1, BSE, EPS1) = 0, 1, 2, 3, 4, 5, 6, 7, 8, 11, 14, 16, 17
NVEC = 18

SROWS = 96
SQ_MASK, LIN_ONE, A_MUL, A_ADD, B_MUL, B_ADD = range(6)


def shape_constants():
    c = np.zeros((P, P + 6), np.float32)
    c[:, :P] = np.eye(P, dtype=np.float32)
    for q in range(3):
        for j in range(3):
            for i in range(NSE):
                r = 32 * q + NSE * j + i
                c[r, P + SQ_MASK] = j > 0
                c[r, P + LIN_ONE] = j == 0
                c[r, P + A_MUL] = (2.0, 0.0, 1.0)[j]
                c[r, P + A_ADD] = -1.0 if j == 1 and q != 0 else 0.0
                c[r, P + B_MUL] = (1.0, 1.0, 0.0)[j]
                c[r, P + B_ADD] = -1.0 if j == 2 and q != 2 else 0.0
    return c


def laid_out(a):
    f = {n: np.asarray(v) for n, v in a.items()}
    o = {}
    o["x"] = f["x"].reshape(GROUPS, GB, T, PAR, D).transpose(0, 4, 1, 3, 2)
    o["adj"] = f["adj"].reshape(GROUPS, GB, T, PAR, T, PAR).transpose(0, 4, 1, 5, 3, 2)
    se = np.zeros((P, SROWS), np.float32)
    bse = np.zeros((P,), np.float32)
    for q in range(3):
        for j in range(3):
            r = 32 * q + NSE * j
            se[:, r:r + NSE] = f["L0_gnn_w_se"].T
            bse[r:r + NSE] = f["L0_gnn_b_se"]
    bn = [f[f"L0_gnn_bn{k}_{v}"] for k in (1, 2) for v in "gbmv"]
    vec = np.stack(bn + list(f["L0_gnn_b_ih"].reshape(3, P)) + list(f["L0_gnn_b_hh"].reshape(3, P))
                   + list(f["L1_gnn_b1"].reshape(2, P)) + [bse, np.repeat(f["L1_gnn_eps"], P)], axis=1)
    o["first"] = np.concatenate([vec, f["L0_gnn_conv1_w"][:, :, 0].T, se,
                                ], axis=1)
    o["conv2"] = f["L0_gnn_conv2_w"].transpose(1, 2, 0)
    ih = f["L0_gnn_w_ih"].reshape(3, P, 2, P).transpose(3, 2, 0, 1)
    hh = f["L0_gnn_w_hh"].reshape(3, P, P).transpose(2, 0, 1)
    o["gates"] = np.concatenate([hh, ih[:, 1], ih[:, 0]], axis=1)
    o["later"] = np.concatenate([f["L0_gnn_w_msg"].T, f["L1_gnn_W1"],
                                 f["L1_gnn_W2"].reshape(2, P, D).transpose(1, 0, 2).reshape(P, 2 * D),
                                 np.tile(f["L0_gnn_b_msg"], (P, 1)), np.tile(f["L1_gnn_b2"], (P, 1))], axis=1)
    o["consts"] = shape_constants()
    return {n: np.ascontiguousarray(v) for n, v in o.items()}


def gnn_kernel(nc, t, out):
    fp32 = mybir.dt.float32
    f32r = mybir.dt.float32r
    ALU = mybir.AluOpType
    ACT = mybir.ActivationFunctionType

    x_v = t["x"].rearrange("g d b r t -> g d (b r t)")
    adj_v = t["adj"].rearrange("g m b r q n -> g m (b r q n)")
    out_v = out.rearrange("(g h b) (t r) d -> g h t b (r d)", h=PAIRS, b=GB // PAIRS, r=PAR)

    ctx = ExitStack()
    with ctx:
        def sb(name, shape, dt=fp32):
            return ctx.enter_context(nc.sbuf_tensor(name, shape, dt))

        def sem(name):
            return ctx.enter_context(nc.semaphore(name))

        cst = sb("cst", [P, P + 6])
        ident = cst[:, 0:P]
        first_w = sb("first_w", [P, NVEC + P + SROWS])
        vec = first_w[:, 0:NVEC]
        c1raw = first_w[:, NVEC:NVEC + P]
        seraw = first_w[:, NVEC + P:NVEC + P + SROWS]
        later_w = sb("later_w", [P, P + HID + 2 * D + 2 * P])
        wmsgT = later_w[:, 0:P]
        w1raw = later_w[:, P:P + HID]
        w2 = later_w[:, P + HID:P + HID + 2 * D].rearrange("p (f d) -> p f d", d=D)
        bmsg = later_w[:, P + HID + 2 * D:2 * P + HID + 2 * D]
        b2bc = later_w[:, 2 * P + HID + 2 * D:3 * P + HID + 2 * D]
        rs = sb("rs", [P, 2])
        ones = sb("ones", [P, P])
        three = sb("three", [P, 1])
        bn2_diag = sb("bn2_diag", [P, P])
        bn2_row = sb("bn2_row", [P, P])
        bn = sb("bn", [P, 6])
        gbias = sb("gbias", [P, 4])
        sescale = sb("sescale", [SROWS, 1])
        minus_half = sb("minus_half", [P, BLK])
        epst = sb("epst", [P, 2, BLK])
        diag = sb("diag", [P, P])
        wh = sb("wh", [P, NSLOT, P], f32r)
        wl = sb("wl", [P, NSLOT, P], f32r)
        w1h = sb("w1h", [P, HID], f32r)
        w1l = sb("w1l", [P, HID], f32r)
        wseh = sb("wseh", [P, SROWS], f32r)
        wsel = sb("wsel", [P, SROWS], f32r)

        xv = [sb(f"xv{i}", [P, COLS]) for i in range(2)]
        xh = [sb(f"xh{i}", [P, COLS], f32r) for i in range(2)]
        xl = [sb(f"xl{i}", [P, COLS], f32r) for i in range(2)]
        sv = sb("sv", [SROWS, PAIRS, PC])
        sA = sb("sA", [SROWS, PAIRS, PC], f32r)
        sB = sb("sB", [SROWS, PAIRS, PC], f32r)
        msg = sb("msg", [P, PAIRS, BLK, D])
        adjT = [sb(f"adjT{i}", [P, GB, PAR, N]) for i in range(2)]
        amat = sb("amat", [P, GB, PAR, N])
        nmph = sb("nmph", [P, COLS], f32r)
        nmpl = sb("nmpl", [P, COLS], f32r)
        h1 = sb("h1", [P, GB, PAR, TL])
        dv = sb("dv", [P, 2, GB, TL])
        sth = sb("sth", [P, 3, GB, TL], f32r)
        stl = sb("stl", [P, 3, GB, TL], f32r)
        usum = sb("usum", [P, GB, PAR, T])
        pre = sb("pre", [P, GB, PAR, T])
        xch = sb("xch", [P, GB, PAR, T], f32r)
        xcl = sb("xcl", [P, GB, PAR, T], f32r)
        tr = sb("tr", [P, PAIRS, PC])
        tz = sb("tz", [P, PAIRS, PC])
        ghn = sb("ghn", [P, PAIRS, PC])
        gwork = sb("gwork", [P, 2, PAIRS, PC])
        nn, xw = gwork[:, 0, :, :], gwork[:, 1, :, :]
        stats = sb("stats", [P, 2, PAIRS, BLK, 6])
        mv = sb("mv", [P, 2, PAIRS, BLK, 2])
        rstd = sb("rstd", [P, 2, PAIRS, BLK])
        xn = sb("xn", [P, PAIRS, BLK, D])
        hh = sb("hh", [P, PAIRS, PC], f32r)
        hl = sb("hl", [P, PAIRS, PC], f32r)
        tail = sb("tail", [P, (HID // P + 1) * COLS])
        hid = tail[:, 0:HID // P * COLS].rearrange("p (h f n) -> p h f n", h=PAIRS, f=HID // P)
        ot = tail[:, HID // P * COLS:].rearrange("p (h k d) -> p h k d", h=PAIRS, k=BLK)

        c2raw = tail[:, 0:TAPS * P].rearrange("p (k o) -> p k o", k=TAPS)
        msum = gwork[:, :, :, :].rearrange("p a h n -> p (a h n)")[:, 0:NM * P].rearrange("p (k o) -> p k o", k=NM)
        graw = adjT[1][:, :, :, :].rearrange("p b r n -> p (b r n)")[:, 0:9 * P].rearrange("p (k o) -> p k o", k=9)

        fb = [ctx.enter_context(nc.psum_tensor(f"front{i}", [P, PC], fp32)) for i in range(2)]
        bb = [ctx.enter_context(nc.psum_tensor(f"back{i}", [P, PC], fp32)) for i in range(3)]
        cb = [ctx.enter_context(nc.psum_tensor(f"conv{i}", [P, PC], fp32)) for i in range(3)]

        count = {}

        def stage(name, per_group):
            count[name] = (sem(name), per_group)
            return name

        X_LOADED = stage("x_loaded", 16)
        ADJ_LOADED = stage("adj_loaded", 16)
        STORED = [stage(f"out{h}_stored", 16) for h in range(PAIRS)]
        XH_READY = stage("xh_ready", 2)
        XL_READY = stage("xl_ready", 2)
        C1_FULL = stage("conv1_full", 2)
        H1_READY = stage("h1_ready", 2)
        DV_READY = stage("h1_diff_ready", 2)
        STH_READY = stage("stream_high_ready", 3)
        ST_READY = [stage(f"stream{n}_ready", 1) for n in "MAB"]
        CONV_FULL = [stage(f"conv{n}_full", 1) for n in "MAB"]
        U_READY = stage("usum_ready", 2)
        PRE_READY = stage("pre_ready", 2)
        XCH_READY = stage("xconv_high_ready", 2)
        XCL_READY = stage("xconv_low_ready", 2)
        S_FULL = stage("se_full", 2)
        SV_READY = stage("sv_ready", 2)
        SW_READY = stage("sw_ready", 2)
        SHI_READY = stage("s_high_ready", 2)
        SLO_READY = stage("s_low_ready", 2)
        MSG_FULL = stage("msg_full", 2)
        MSUM_READY = stage("msg_sum_ready", 2)
        MSG_READY = stage("msg_ready", 2)
        DIST_FULL = stage("dist_full", 4)
        E_READY = stage("exp_ready", 4)
        A_READY = stage("a_ready", 4)
        ADJE_READY = stage("adjT_eps_ready", 4)
        NMP_FULL = stage("nmp_full", 2)
        NH_READY = stage("nmp_high_ready", 2)
        NL_READY = stage("nmp_low_ready", 2)
        R_FULL = stage("gate_r_full", 2)
        HN_FULL = stage("gate_hn_full", 2)
        IN_FULL = stage("gate_in_full", 2)
        Z_FULL = stage("gate_z_full", 2)
        TR_READY = stage("tr_ready", 2)
        GHN_READY = stage("ghn_ready", 2)
        T1_READY = stage("t1_ready", 2)
        T2_READY = stage("t2_ready", 2)
        N_READY = stage("n_ready", 2)
        TZ_READY = stage("tz_ready", 2)
        XW_READY = stage("x_weight_ready", 2)
        XWX_READY = stage("weighted_x_ready", 2)
        F_READY = stage("f_ready", 2)
        Y2_READY = stage("y2_ready", 2)
        Y_FULL = stage("y_full", 2)
        STATS = [stage(f"stats{k}_ready", 2) for k in (1, 2)]
        MV = [stage(f"mv{k}_ready", 2) for k in (1, 2)]
        VE = [stage(f"var_eps{k}_ready", 2) for k in (1, 2)]
        RSTD = [stage(f"rstd{k}_ready", 2) for k in (1, 2)]
        XN_READY = stage("xn_ready", 2)
        XNB_READY = stage("xnb_ready", 2)
        AGG_FULL = stage("agg_full", 2)
        HH_READY = stage("h_high_ready", 2)
        HL_READY = stage("h_low_ready", 2)
        W1_FULL = stage("w1_full", 4)
        HID_READY = stage("hid_ready", 4)
        W2_FULL = stage("w2_full", 2)
        V_READY = stage("v_ready", 2)
        OT_READY = stage("out_ready", 2)

        consts_loaded = sem("consts_loaded")
        first_loaded = sem("first_loaded")
        conv2_loaded = sem("conv2_loaded")
        gates_loaded = sem("gates_loaded")
        later_loaded = sem("later_loaded")
        exponent_set = sem("exponent_set")
        pads_zeroed = sem("pads_zeroed")
        bn_var_ready = sem("bn_var_ready")
        bn_rsqrt_ready = sem("bn_rsqrt_ready")
        bn_ready = sem("bn_ready")
        prep_chain = sem("prep_chain")
        bn2_row_full = sem("bn2_row_full")
        w_scaled = sem("w_scaled")
        w_high = sem("w_high")
        w_low = sem("w_low")

        def wait(eng, name, g, j):
            s, per = count[name]
            v = g * per + j
            if not (isinstance(v, int) and v <= 0):
                eng.wait_ge(s, v)

        def done(ins, name):
            s, per = count[name]
            ins.then_inc(s, 16 if per == 16 else 1)

        def blocks(ap):
            return ap.rearrange("p (k c) -> p k c", c=P)

        def flat(ap):
            return ap.rearrange("p b r n -> p (b r n)")

        def full(ap):
            return ap.bitcast(fp32)

        def cols(h):
            return slice(h * PC, (h + 1) * PC)

        def gate_bank(h, k):
            return bb[(4 * h + k) % 3][:, :]

        def back_bank(n):
            return bb[n % 3][:, :]

        Y_TILE, AGG_TILE, HID_TILE, OUT_TILE = 8, 10, 12, 16

        def run(eng, prologue, steady, last):
            prologue()
            steady(1, 1, True)
            with eng.Fori(0, (GROUPS - 4) // 2) as i:
                steady(i * 2 + 2, 0, True)
                steady(i * 2 + 3, 1, True)
            steady(GROUPS - 2, 0, True)
            steady(GROUPS - 1, 1, False)
            last(GROUPS - 1, (GROUPS - 1) % 2)

        block = ctx.enter_context(nc.Block())

        @block.sync
        def _(sp):
            def load_x(g, u):
                done(sp.dma_start(xv[u][:, :], x_v[g, :, :]), X_LOADED)

            def load_adj(g, u):
                done(sp.dma_start(flat(adjT[u][:, :, :, :]), adj_v[g, :, :]), ADJ_LOADED)

            def store(g):
                for h in range(PAIRS):
                    wait(sp, OT_READY, g, h + 1)
                    done(sp.dma_start(out_v[g, h, :, :, :], ot[:, h, :, :].rearrange("p (b r) d -> p b (r d)", r=PAR)),
                         STORED[h])

            def prologue():
                sp.dma_start(first_w[:, :], t["first"]).then_inc(first_loaded, 16)
                load_x(0, 0)
                sp.dma_start(c2raw, t["conv2"]).then_inc(conv2_loaded, 16)
                sp.dma_start(later_w[:, :], t["later"]).then_inc(later_loaded, 16)
                load_adj(0, 0)
                sp.dma_start(graw, t["gates"]).then_inc(gates_loaded, 16)
                wait(sp, X_LOADED, 0, 16)
                load_x(1, 1)
                wait(sp, ADJ_LOADED, 0, 16)
                sp.wait_ge(w_low, 5)
                load_adj(1, 1)

            def steady(s, u, front):
                gb = s - 1
                if front:
                    wait(sp, XWX_READY, gb, 2)
                    load_x(s + 1, 1 - u)
                    wait(sp, AGG_FULL, gb, 2)
                    wait(sp, A_READY, s, 1)
                    load_adj(s + 1, 1 - u)
                store(gb)

            def last(g, u):
                store(g)
                for h in range(PAIRS):
                    wait(sp, STORED[h], g, 16)

            run(sp, prologue, steady, last)

        @block.gpsimd
        def _(pool):
            def differences(g):
                wait(pool, H1_READY, g, 2)
                wait(pool, ST_READY[1], g - 1, 1)
                done(pool.tensor_tensor(dv[:, 0, :, :], h1[:, :, 0, :], h1[:, :, 1, :], ALU.subtract), DV_READY)
                wait(pool, ST_READY[2], g - 1, 1)
                done(pool.tensor_tensor(dv[:, 1, :, 0:TL - 1], h1[:, :, 0, 1:TL], h1[:, :, 1, 0:TL - 1],
                                        ALU.subtract), DV_READY)

            def rsqrt(k, g, h):
                wait(pool, MV[k], g, h + 1)
                done(pool.tensor_tensor(rstd[:, k, h, :], mv[:, k, h, :, 1], epst[:, k, :], ALU.add), VE[k])
                wait(pool, VE[k], g, h + 1)
                done(pool.tensor_tensor(rstd[:, k, h, :], rstd[:, k, h, :], minus_half[:, :], ALU.pow), RSTD[k])

            def residual(g, u):
                for h in range(PAIRS):
                    wait(pool, XW_READY, g, h + 1)
                    done(pool.tensor_tensor(xw[:, h, :], xw[:, h, :], xv[u][:, cols(h)], ALU.mult), XWX_READY)

            def add_b2(g, h):
                wait(pool, XN_READY, g, h + 1)
                wait(pool, STORED[h], g - 1, 16)
                done(pool.tensor_tensor(ot[:, h, :, :], xn[:, h, :, :],
                                        b2bc.unsqueeze(1).to_broadcast([P, BLK, D]), ALU.add), XNB_READY)

            def mask(g, u, b):
                wait(pool, E_READY, g, b + 1)
                wait(pool, ADJ_LOADED, g, 16)
                done(pool.tensor_tensor(amat[:, b, :, :], amat[:, b, :, :], adjT[u][:, b, :, :], ALU.mult), A_READY)

            def add_diagonal(g, u, b):
                a = adjT[u][:, b, :, :].rearrange("p r n -> p (r n)")
                dg = bass.AP(a.tensor, a.offset, [a.ap[0], [N + P, PAR], [1, P]])
                wait(pool, A_READY, g, b + 1)
                done(pool.tensor_tensor(dg, dg, diag[:, :].unsqueeze(1).to_broadcast([P, PAR, P]), ALU.add), ADJE_READY)

            def prologue():
                pool.memset(minus_half[:, :], -0.5).then_inc(exponent_set, 1)
                pool.memset(ones[:, :], 1.0).then_inc(exponent_set, 1)
                pool.memset(three[:, :], 3.0)
                pool.memset(h1[:, :, :, :], 0.0).then_inc(pads_zeroed, 1)
                pool.memset(dv[:, :, :, :], 0.0).then_inc(pads_zeroed, 1)
                pool.memset(epst[:, 0, :], 4 * EPS).then_inc(pads_zeroed, 1)
                pool.memset(epst[:, 1, :], EPS).then_inc(pads_zeroed, 1)
                pool.wait_ge(exponent_set, 1)
                pool.wait_ge(bn_var_ready, 1)
                pool.tensor_tensor(rs[:, :], rs[:, :], minus_half[:, 0:2], ALU.pow).then_inc(bn_rsqrt_ready, 1)
                pool.wait_ge(pads_zeroed, 4)
                differences(0)
                for b in range(GB):
                    mask(0, 0, b)
                pool.wait_ge(bn_ready, 4)
                for b in range(GB):
                    add_diagonal(0, 0, b)
                differences(1)

            def steady(s, u, front):
                gb, gm = s - 1, s
                residual(gb, 1 - u)
                rsqrt(0, gb, 0)
                rsqrt(0, gb, 1)
                add_b2(gb, 0)
                add_b2(gb, 1)
                for b in range(GB):
                    mask(gm, u, b)
                rsqrt(1, gb, 0)
                rsqrt(1, gb, 1)
                for b in range(GB):
                    add_diagonal(gm, u, b)
                if front:
                    differences(s + 1)

            def last(g, u):
                residual(g, u)
                rsqrt(0, g, 0)
                rsqrt(0, g, 1)
                add_b2(g, 0)
                add_b2(g, 1)
                rsqrt(1, g, 0)
                rsqrt(1, g, 1)

            run(pool, prologue, steady, last)

        @block.scalar
        def _(act):
            def high(dst, src, name):
                done(act.activation(dst, src, ACT.Copy), name)

            def x_high(g, u):
                wait(act, X_LOADED, g, 16)
                for h in range(PAIRS):
                    high(xh[u][:, cols(h)], xv[u][:, cols(h)], XH_READY)

            def h1_out(g, h):
                if h == 0:
                    wait(act, DV_READY, g - 1, 2)
                    wait(act, ST_READY[0], g - 1, 1)
                wait(act, C1_FULL, g, h + 1)
                done(act.activation(h1[:, 2 * h:2 * h + 2, :, PAD:PAD + T].rearrange("p b r t -> p (b r) t"),
                                    blocks(fb[h][:, :]), ACT.Relu, bias=bn[:, 2:3], scale=bn[:, 0:1]), H1_READY)

            def se_values(g, h):
                wait(act, S_FULL, g, h + 1)
                done(act.activation(sv[:, h, :], fb[h][0:SROWS, :], ACT.Identity,
                                    bias=sescale[:, 0:1], scale=cst[0:SROWS, P + SQ_MASK:P + SQ_MASK + 1]), SV_READY)

            def se_high(g, h):
                wait(act, SW_READY, g, h + 1)
                act.activation(sA[:, h, :], sv[:, h, :], ACT.Identity,
                               bias=cst[0:SROWS, P + A_ADD:P + A_ADD + 1], scale=cst[0:SROWS, P + A_MUL:P + A_MUL + 1])
                done(act.activation(sB[:, h, :], sv[:, h, :], ACT.Identity,
                                    bias=cst[0:SROWS, P + B_ADD:P + B_ADD + 1],
                                    scale=cst[0:SROWS, P + B_MUL:P + B_MUL + 1]), SHI_READY)

            def exps(g, b):
                wait(act, DIST_FULL, g, b + 1)
                done(act.activation(amat[:, b, :, :].rearrange("p r n -> p (r n)"), fb[b % 2][:, :], ACT.Exp), E_READY)

            def nmp_high(g, h):
                wait(act, NMP_FULL, g, h + 1)
                high(nmph[:, cols(h)], fb[h][:, :], NH_READY)

            def gates(g, h):
                wait(act, HN_FULL, g, h + 1)
                done(act.activation(ghn[:, h, :], gate_bank(h, 1), ACT.Identity, bias=gbias[:, 2:3], scale=0.5), GHN_READY)
                wait(act, R_FULL, g, h + 1)
                done(act.activation(tr[:, h, :], gate_bank(h, 0), ACT.Tanh, bias=gbias[:, 0:1], scale=0.5), TR_READY)
                wait(act, Z_FULL, g, h + 1)
                done(act.activation(tz[:, h, :], gate_bank(h, 2), ACT.Tanh, bias=gbias[:, 1:2], scale=0.5), TZ_READY)
                wait(act, TZ_READY, g, h + 1)
                done(act.activation(xw[:, h, :], tz[:, h, :], ACT.Identity, bias=three[:, 0:1]), XW_READY)
                act.activation(tz[:, h, :], tz[:, h, :], ACT.Identity, bias=ones[:, 0:1], scale=-1.0)
                wait(act, T2_READY, g, h + 1)
                done(act.activation(nn[:, h, :], ghn[:, h, :], ACT.Tanh, bias=gbias[:, 3:4]), N_READY)

            def xconv_high(g, par):
                wait(act, PRE_READY, g, par + 1)
                high_relu = act.activation(xch[:, :, par, :], pre[:, :, par, :], ACT.Relu)
                done(high_relu, XCH_READY)

            def h_high(g, h):
                wait(act, AGG_FULL, g, h + 1)
                high(hh[:, h, :], back_bank(AGG_TILE + h), HH_READY)

            def hidden(g, h):
                for f in range(2):
                    wait(act, W1_FULL, g, 2 * h + f + 1)
                    done(act.activation(hid[:, h, f, :], back_bank(HID_TILE + 2 * h + f), ACT.Relu,
                                        bias=vec[:, B1 + f:B1 + f + 1]), HID_READY)

            def prologue():
                act.dma_start(cst[:, :], t["consts"]).then_inc(consts_loaded, 16)
                act.wait_ge(first_loaded, 16)
                act.activation(wh[:, 0, :], c1raw, ACT.Copy)
                act.activation(wseh[:, :], seraw, ACT.Copy).then_inc(w_high, 1)
                x_high(0, 0)
                act.wait_ge(pads_zeroed, 4)
                act.wait_ge(bn_ready, 1)
                h1_out(0, 0)
                h1_out(0, 1)
                act.wait_ge(w_scaled, 1)
                act.activation(wh[:, S_M:S_M + NM, :], msum, ACT.Copy).then_inc(w_high, 1)
                act.wait_ge(bn_ready, 4)
                for h in range(PAIRS):
                    se_values(0, h)
                act.wait_ge(w_scaled, 2)
                act.activation(wh[:, S_A:S_A + NP_, :], c2raw[:, 0:TAPS:2, :], ACT.Copy).then_inc(w_high, 1)
                for h in range(PAIRS):
                    se_high(0, h)
                act.wait_ge(w_scaled, 3)
                act.activation(wh[:, S_B:S_B + NR, :], c2raw[:, 1:TAPS:2, :], ACT.Copy).then_inc(w_high, 1)
                for b in range(GB):
                    exps(0, b)
                x_high(1, 1)
                act.wait_ge(gates_loaded, 16)
                act.activation(wh[:, S_GATE:S_GATE + 9, :], graw, ACT.Copy).then_inc(w_high, 1)
                act.activation(w1h[:, :], w1raw, ACT.Copy).then_inc(w_high, 1)
                nmp_high(0, 0)
                nmp_high(0, 1)
                xconv_high(0, 0)
                h1_out(1, 0)
                h1_out(1, 1)
                xconv_high(0, 1)

            def steady(s, u, front):
                gb, gm, gf = s - 1, s, s + 1
                se_values(gm, 0)
                se_values(gm, 1)
                se_high(gm, 0)
                se_high(gm, 1)
                gates(gb, 0)
                gates(gb, 1)
                if front:
                    x_high(gf, 1 - u)
                h_high(gb, 0)
                h_high(gb, 1)
                exps(gm, 0)
                exps(gm, 1)
                hidden(gb, 0)
                exps(gm, 2)
                exps(gm, 3)
                hidden(gb, 1)
                nmp_high(gm, 0)
                nmp_high(gm, 1)
                xconv_high(gm, 0)
                if front:
                    h1_out(gf, 0)
                    h1_out(gf, 1)
                xconv_high(gm, 1)

            def last(g, u):
                gates(g, 0)
                gates(g, 1)
                h_high(g, 0)
                h_high(g, 1)
                hidden(g, 0)
                hidden(g, 1)

            run(act, prologue, steady, last)

        @block.vector
        def _(dve):
            def low(dst, src, hi, name):
                done(dve.tensor_tensor(dst, src, full(hi), ALU.subtract), name)

            def x_low(g, u, h):
                wait(dve, XH_READY, g, h + 1)
                low(xl[u][:, cols(h)], xv[u][:, cols(h)], xh[u][:, cols(h)], XL_READY)

            def split(g, st):
                src = (h1[:, :, 1, :], dv[:, 0, :, :], dv[:, 1, :, :])[st]
                if st == 0:
                    wait(dve, H1_READY, g, 2)
                else:
                    wait(dve, DV_READY, g, st)
                wait(dve, CONV_FULL[st], g - 1, 1)
                done(dve.tensor_copy(sth[:, st, :, :], src), STH_READY)
                wait(dve, STH_READY, g, st + 1)
                low(stl[:, st, :, :], src, sth[:, st, :, :], ST_READY[st])

            def se_rows(g, h):
                wait(dve, SV_READY, g, h + 1)
                done(dve.scalar_tensor_tensor(sv[:, h, :], fb[h][0:SROWS, :], vec[0:SROWS, BSE:BSE + 1], sv[:, h, :],
                                              ALU.add, ALU.mult), SW_READY)

            def se_low(g, h):
                wait(dve, SHI_READY, g, h + 1)
                dve.scalar_tensor_tensor(sA[0:32, h, :], sv[0:32, h, :], cst[0:32, P + A_MUL:P + A_MUL + 1],
                                         full(sA[0:32, h, :]), ALU.mult, ALU.subtract)
                done(dve.scalar_tensor_tensor(sB[64:96, h, :], sv[64:96, h, :], cst[64:96, P + B_MUL:P + B_MUL + 1],
                                              full(sB[64:96, h, :]), ALU.mult, ALU.subtract), SLO_READY)

            def messages(g, h):
                wait(dve, MSG_FULL, g, h + 1)
                done(dve.tensor_tensor(msg[:, h, :, :], blocks(fb[h][:, :]),
                                       bmsg.unsqueeze(1).to_broadcast([P, BLK, D]), ALU.add), MSUM_READY)
                wait(dve, MSUM_READY, g, h + 1)
                done(dve.tensor_scalar(msg[:, h, :, :], msg[:, h, :, :], 0.0, None, ALU.max), MSG_READY)

            def nmp_low(g, h):
                wait(dve, NH_READY, g, h + 1)
                low(nmpl[:, cols(h)], fb[h][:, :], nmph[:, cols(h)], NL_READY)

            def shared_sum(g, u):
                wait(dve, CONV_FULL[0], g, 1)
                xs = xv[u][:, :].rearrange("p (b r t) -> p b r t", b=GB, r=PAR)
                m = cb[0][:, :].rearrange("p (b t) -> p b t", t=T)
                for par in range(PAR):
                    done(dve.tensor_tensor(usum[:, :, par, :], m, xs[:, :, par, :], ALU.add), U_READY)

            def pre_sum(g, par):
                wait(dve, CONV_FULL[1 + par], g, 1)
                wait(dve, U_READY, g, par + 1)
                done(dve.scalar_tensor_tensor(pre[:, :, par, :], cb[1 + par][:, :].rearrange("p (b t) -> p b t", t=T),
                                              bn[:, 5:6], usum[:, :, par, :], ALU.add, ALU.add), PRE_READY)

            def xconv_low(g, par):
                wait(dve, XCH_READY, g, par + 1)
                done(dve.scalar_tensor_tensor(xcl[:, :, par, :], pre[:, :, par, :], 0.0, full(xch[:, :, par, :]),
                                              ALU.max, ALU.subtract), XCL_READY)

            def gates(g, u, h):
                wait(dve, GHN_READY, g, h + 1)
                wait(dve, TR_READY, g, h + 1)
                done(dve.scalar_tensor_tensor(ghn[:, h, :], tr[:, h, :], 1.0, ghn[:, h, :], ALU.add, ALU.mult), T1_READY)
                wait(dve, IN_FULL, g, h + 1)
                wait(dve, T1_READY, g, h + 1)
                done(dve.tensor_tensor(ghn[:, h, :], gate_bank(h, 3), ghn[:, h, :], ALU.add), T2_READY)

            def gates_end(g, h):
                wait(dve, N_READY, g, h + 1)
                done(dve.tensor_tensor(tr[:, h, :], tz[:, h, :], nn[:, h, :], ALU.mult), F_READY)
                wait(dve, XWX_READY, g, h + 1)
                wait(dve, F_READY, g, h + 1)
                done(dve.tensor_tensor(tr[:, h, :], tr[:, h, :], xw[:, h, :], ALU.add), Y2_READY)

            def norm_stats(k, g, h, src):
                for q in range(BLK):
                    last = dve.bn_stats(stats[:, k, h, q, :], src(q))
                done(last, STATS[k])
                wait(dve, STATS[k], g, h + 1)
                dve.nop(nofuse=True)
                for q in range(BLK):
                    last = dve.bn_aggr(mv[:, k, h, q, :], stats[:, k, h, q, :])
                done(last, MV[k])

            def norm_apply(k, g, h, src, dst, ready):
                wait(dve, RSTD[k], g, h + 1)
                for q in range(BLK):
                    last = dve.tensor_scalar(dst(q), src(q), mv[:, k, h, q, 0:1], rstd[:, k, h, q:q + 1],
                                             ALU.subtract, ALU.mult)
                done(last, ready)

            def y_block(h):
                bank = back_bank(Y_TILE + h)
                return lambda q: bank[:, q * P:(q + 1) * P]

            def y_stats(g, h):
                wait(dve, Y_FULL, g, h + 1)
                norm_stats(0, g, h, y_block(h))

            def y_apply(g, h):
                norm_apply(0, g, h, y_block(h), lambda q: xn[:, h, q, :], XN_READY)

            def h_low(g, h):
                wait(dve, HH_READY, g, h + 1)
                low(hl[:, h, :], back_bank(AGG_TILE + h), hh[:, h, :], HL_READY)

            def out_stats(g, h):
                wait(dve, W2_FULL, g, h + 1)
                wait(dve, XNB_READY, g, h + 1)
                row = ot[:, h, :, :].rearrange("p k d -> p (k d)")
                done(dve.tensor_tensor(row, back_bank(OUT_TILE + h), row, ALU.add), V_READY)
                wait(dve, V_READY, g, h + 1)
                norm_stats(1, g, h, lambda q: ot[:, h, q, :])

            def out_apply(g, h):
                norm_apply(1, g, h, lambda q: ot[:, h, q, :], lambda q: ot[:, h, q, :], OT_READY)

            def prologue():
                n = [0]

                def link(ins):
                    n[0] += 1
                    ins.then_inc(prep_chain, 1)
                    dve.wait_ge(prep_chain, n[0])

                def w_low_part(dst, src, hi, k):
                    dve.wait_ge(w_high, k)
                    dve.tensor_tensor(dst, src, full(hi), ALU.subtract).then_inc(w_low, 1)

                dve.wait_ge(first_loaded, 16)
                dve.tensor_scalar(rs[:, 0:1], vec[:, BN1_V:BN1_V + 1], EPS, None, ALU.add)
                dve.tensor_scalar(rs[:, 1:2], vec[:, BN2_V:BN2_V + 1], EPS, None, ALU.add).then_inc(bn_var_ready, 1)
                dve.wait_ge(w_high, 1)
                dve.tensor_tensor(wsel[:, :], seraw, full(wseh[:, :]), ALU.subtract)
                w_low_part(wl[:, 0, :], c1raw, wh[:, 0, :], 1)
                dve.wait_ge(bn_rsqrt_ready, 1)
                for k in range(2):
                    c = 3 * k
                    link(dve.tensor_tensor(bn[:, c:c + 1], rs[:, k:k + 1], vec[:, 4 * k:4 * k + 1], ALU.mult))
                    link(dve.tensor_tensor(bn[:, c + 1:c + 2], bn[:, c:c + 1], vec[:, 4 * k + 2:4 * k + 3], ALU.mult))
                    ins = dve.tensor_tensor(bn[:, c + 2:c + 3], vec[:, 4 * k + 1:4 * k + 2], bn[:, c + 1:c + 2], ALU.subtract)
                ins.then_inc(bn_ready, 1)
                dve.wait_ge(consts_loaded, 16)
                dve.tensor_scalar(bn2_diag[:, :], ident, bn[:, 3:4], None, ALU.mult).then_inc(bn_ready, 1)
                x_low(0, 0, 0)
                x_low(0, 0, 1)
                link(dve.scalar_tensor_tensor(sescale[:, :], vec[0:SROWS, BSE:BSE + 1],
                                              cst[0:SROWS, P + SQ_MASK:P + SQ_MASK + 1],
                                              cst[0:SROWS, P + LIN_ONE:P + LIN_ONE + 1], ALU.mult, ALU.add))
                link(dve.tensor_tensor(gbias[:, 0:3], vec[:, BIH:BIH + 3], vec[:, BHH:BHH + 3], ALU.add))
                link(dve.tensor_scalar(gbias[:, 0:2], gbias[:, 0:2], 0.5, None, ALU.mult))
                dve.tensor_scalar(gbias[:, 2:3], vec[:, BHH + 2:BHH + 3], 0.5, None, ALU.mult)
                dve.tensor_copy(gbias[:, 3:4], vec[:, BIH + 2:BIH + 3]).then_inc(bn_ready, 1)
                dve.scalar_tensor_tensor(diag[:, :], ident, vec[:, EPS1:EPS1 + 1], ident, ALU.mult, ALU.add).then_inc(bn_ready, 1)
                dve.wait_ge(bn2_row_full, 1)
                dve.tensor_copy(bn2_row[:, :], cb[2][:, 0:P])
                dve.wait_ge(conv2_loaded, 16)
                dve.tensor_tensor(msum[:, 0:NM - 1, :], c2raw[:, 0:TAPS - 1:2, :], c2raw[:, 1:TAPS:2, :], ALU.add)
                link(dve.tensor_copy(msum[:, NM - 1, :], c2raw[:, TAPS - 1, :]))
                scale = bn2_row[:, :].unsqueeze(1)
                dve.tensor_tensor(msum[:, :, :], msum[:, :, :], scale.to_broadcast([P, NM, P]), ALU.mult).then_inc(w_scaled, 1)
                split(0, 0)
                w_low_part(wl[:, S_M:S_M + NM, :], msum, wh[:, S_M:S_M + NM, :], 2)
                se_rows(0, 0)
                se_rows(0, 1)
                dve.tensor_tensor(c2raw[:, 0:TAPS:2, :], c2raw[:, 0:TAPS:2, :], scale.to_broadcast([P, NP_, P]),
                                  ALU.mult).then_inc(w_scaled, 1)
                dve.wait_ge(later_loaded, 16)
                messages(0, 0)
                messages(0, 1)
                split(0, 1)
                w_low_part(wl[:, S_A:S_A + NP_, :], c2raw[:, 0:TAPS:2, :], wh[:, S_A:S_A + NP_, :], 3)
                dve.tensor_tensor(c2raw[:, 1:TAPS:2, :], c2raw[:, 1:TAPS:2, :], scale.to_broadcast([P, NR, P]),
                                  ALU.mult).then_inc(w_scaled, 1)
                se_low(0, 0)
                se_low(0, 1)
                split(0, 2)
                w_low_part(wl[:, S_B:S_B + NR, :], c2raw[:, 1:TAPS:2, :], wh[:, S_B:S_B + NR, :], 4)
                shared_sum(0, 0)
                x_low(1, 1, 0)
                x_low(1, 1, 1)
                dve.wait_ge(gates_loaded, 16)
                w_low_part(wl[:, S_GATE:S_GATE + 9, :], graw, wh[:, S_GATE:S_GATE + 9, :], 5)
                w_low_part(w1l[:, :], w1raw, w1h[:, :], 6)
                nmp_low(0, 0)
                nmp_low(0, 1)
                pre_sum(0, 0)
                xconv_low(0, 0)
                split(1, 0)
                pre_sum(0, 1)
                split(1, 1)
                xconv_low(0, 1)
                split(1, 2)

            def steady(s, u, front):
                gb, gm, gf = s - 1, s, s + 1
                se_rows(gm, 0)
                se_rows(gm, 1)
                messages(gm, 0)
                messages(gm, 1)
                se_low(gm, 0)
                se_low(gm, 1)
                gates(gb, 1 - u, 0)
                gates_end(gb, 0)
                gates(gb, 1 - u, 1)
                y_stats(gb, 0)
                gates_end(gb, 1)
                y_apply(gb, 0)
                y_stats(gb, 1)
                y_apply(gb, 1)
                shared_sum(gm, u)
                h_low(gb, 0)
                h_low(gb, 1)
                if front:
                    x_low(gf, 1 - u, 0)
                    x_low(gf, 1 - u, 1)
                out_stats(gb, 0)
                out_stats(gb, 1)
                nmp_low(gm, 0)
                out_apply(gb, 0)
                nmp_low(gm, 1)
                out_apply(gb, 1)
                pre_sum(gm, 0)
                xconv_low(gm, 0)
                if front:
                    split(gf, 0)
                pre_sum(gm, 1)
                if front:
                    split(gf, 1)
                xconv_low(gm, 1)
                if front:
                    split(gf, 2)

            def last(g, u):
                gates(g, u, 0)
                gates_end(g, 0)
                gates(g, u, 1)
                y_stats(g, 0)
                gates_end(g, 1)
                y_apply(g, 0)
                y_stats(g, 1)
                y_apply(g, 1)
                h_low(g, 0)
                h_low(g, 1)
                out_stats(g, 0)
                out_stats(g, 1)
                out_apply(g, 0)
                out_apply(g, 1)

            run(dve, prologue, steady, last)

        @block.tensor
        def _(pe):
            def products(bank, terms, first=True, last=True):
                todo = [(a, b) for (ah, al, bh, bl) in terms for (a, b) in ((ah, bh), (ah, bl), (al, bh))]
                for k, (a, b) in enumerate(todo):
                    ins = pe.matmul(bank, a, b, start=first and k == 0, stop=last and k == len(todo) - 1)
                return ins

            def weights(name, k):
                i = SLOT[(name, k)]
                return wh[:, i, :], wl[:, i, :]

            def taps(g, st, k0, k1):
                n = (NM, NP_, NR)[st]
                if k0 == 0:
                    wait(pe, ST_READY[st], g, 1)
                    if st == 0:
                        wait(pe, U_READY, g - 1, 2)
                    else:
                        wait(pe, PRE_READY, g - 1, st)
                bank = cb[st][:, :].rearrange("p (b t) -> p b t", t=T)
                for k in range(k0, k1):
                    ins = products(bank, [weights("MAB"[st], k) + (sth[:, st, :, k:k + T], stl[:, st, :, k:k + T])],
                                   first=k == 0, last=k == n - 1)
                if k1 == n:
                    done(ins, CONV_FULL[st])

            def conv1(g, u, h):
                wait(pe, NL_READY, g - 1, h + 1)
                wait(pe, XL_READY, g, h + 1)
                done(products(fb[h][:, :], [weights("conv1", 0) + (xh[u][:, cols(h)], xl[u][:, cols(h)])]), C1_FULL)

            def embed(g, u, h):
                wait(pe, H1_READY, g, h + 1)
                done(products(fb[h][0:SROWS, :], [(wseh[:, :], wsel[:, :], xh[u][:, cols(h)], xl[u][:, cols(h)])]), S_FULL)

            def messages(g, u, h):
                wait(pe, SW_READY, g, h + 1)
                for q in range(BLK):
                    ins = pe.matmul(fb[h][:, q * P:(q + 1) * P], xv[u][:, h * PC + q * P:h * PC + (q + 1) * P], wmsgT,
                                    start=True, stop=True)
                done(ins, MSG_FULL)

            def distances(g, b):
                if b < 2:
                    wait(pe, MSUM_READY, g, b + 1)
                else:
                    wait(pe, E_READY, g, b - 1)
                wait(pe, SLO_READY, g, b // 2 + 1)
                h, o = b // 2, (b % 2) * N
                for rm in range(PAR):
                    ins = pe.matmul(fb[b % 2][:, rm * N:(rm + 1) * N], sA[:, h, o + rm * P:o + (rm + 1) * P],
                                    sB[:, h, o:o + N], start=True, stop=True)
                done(ins, DIST_FULL)

            def gather(bank, lhs, rhs):
                for b in range(2):
                    for rm in range(PAR):
                        ins = pe.matmul(bank[:, b * N:(b + 1) * N], lhs(b, rm), rhs(b, rm), start=rm == 0, stop=rm == PAR - 1)
                return ins

            def nmp(g, h):
                wait(pe, E_READY, g, h + 3)
                wait(pe, MSG_READY, g, h + 1)
                wait(pe, A_READY, g, 2 * h + 2)
                done(gather(fb[h], lambda b, rm: msg[:, h, 2 * b + rm, :], lambda b, rm: amat[:, 2 * h + b, rm, :]), NMP_FULL)

            def gates(g, u, h):
                xx = (xh[u][:, cols(h)], xl[u][:, cols(h)])
                nm = (nmph[:, cols(h)], nmpl[:, cols(h)])
                xc = (xch[:, 2 * h:2 * h + 2, :, :].rearrange("p b r t -> p (b r t)"),
                      xcl[:, 2 * h:2 * h + 2, :, :].rearrange("p b r t -> p (b r t)"))
                if h == 0:
                    wait(pe, HID_READY, g - 1, 4)
                    wait(pe, NL_READY, g, 2)
                else:
                    wait(pe, GHN_READY, g, 1)
                products(gate_bank(h, 0), [weights("hid", 0) + xx, weights("nmp", 0) + nm], last=False)
                if h == 0:
                    wait(pe, V_READY, g - 1, 2)
                else:
                    wait(pe, TZ_READY, g, 1)
                done(products(gate_bank(h, 1), [weights("hid", 2) + xx]), HN_FULL)
                if h == 0:
                    wait(pe, XCL_READY, g, 2)
                done(products(gate_bank(h, 0), [weights("conv", 0) + xc], first=False), R_FULL)
                if h == 1:
                    wait(pe, T2_READY, g, 1)
                done(products(gate_bank(h, 2), [weights("hid", 1) + xx, weights("nmp", 1) + nm, weights("conv", 1) + xc]), Z_FULL)
                wait(pe, TR_READY, g, h + 1)
                done(products(gate_bank(h, 3), [weights("nmp", 2) + nm, weights("conv", 2) + xc]), IN_FULL)

            def y_transpose(g, h):
                wait(pe, (GHN_READY, TZ_READY)[h], g, 2)
                wait(pe, Y2_READY, g, h + 1)
                for q in range(BLK):
                    ins = pe.transpose(back_bank(Y_TILE + h)[:, q * P:(q + 1) * P], tr[:, h, q * P:(q + 1) * P], ident)
                done(ins, Y_FULL)

            def aggregate(g, u, h):
                if h == 0:
                    wait(pe, T2_READY, g, 2)
                wait(pe, XN_READY, g, h + 1)
                wait(pe, ADJE_READY, g, 2 * h + 2)
                done(gather(back_bank(AGG_TILE + h), lambda b, rm: xn[:, h, 2 * b + rm, :],
                            lambda b, rm: adjT[u][:, 2 * h + b, rm, :]), AGG_FULL)

            def mlp1(g, h):
                for f in range(2):
                    wait(pe, ((XN_READY, HL_READY), (HL_READY, HID_READY))[h][f], g, 2 - f)
                    wait(pe, HL_READY, g, h + 1)
                    done(products(back_bank(HID_TILE + 2 * h + f),
                                  [(w1h[:, f * P:(f + 1) * P], w1l[:, f * P:(f + 1) * P], hh[:, h, :], hl[:, h, :])]), W1_FULL)

            def mlp2(g, h):
                wait(pe, HID_READY, g, 2 * h + 2)
                for q in range(BLK):
                    for f in range(2):
                        ins = pe.matmul(back_bank(OUT_TILE + h)[:, q * P:(q + 1) * P], hid[:, h, f, q * P:(q + 1) * P],
                                        w2[:, f, :], start=f == 0, stop=f == 1)
                done(ins, W2_FULL)

            M, A, B_ = 0, 1, 2

            def prologue():
                pe.wait_ge(exponent_set, 2)
                pe.wait_ge(bn_ready, 2)
                pe.matmul(cb[2][:, 0:P], ones[:, :], bn2_diag[:, :], start=True, stop=True).then_inc(bn2_row_full, 1)
                pe.wait_ge(w_low, 1)
                conv1(0, 0, 0)
                conv1(0, 0, 1)
                embed(0, 0, 0)
                embed(0, 0, 1)
                pe.wait_ge(w_low, 2)
                taps(0, M, 0, 4)
                pe.wait_ge(later_loaded, 16)
                messages(0, 0, 0)
                messages(0, 0, 1)
                taps(0, M, 4, NM)
                pe.wait_ge(w_low, 3)
                taps(0, A, 0, 4)
                distances(0, 0)
                distances(0, 1)
                taps(0, A, 4, 6)
                distances(0, 2)
                distances(0, 3)
                taps(0, A, 6, NP_)
                pe.wait_ge(w_low, 4)
                taps(0, B_, 0, 2)
                nmp(0, 0)
                taps(0, B_, 2, 4)
                nmp(0, 1)
                taps(0, B_, 4, 6)
                conv1(1, 1, 0)
                taps(0, B_, 6, 7)
                conv1(1, 1, 1)
                taps(0, B_, 7, NR)
                pe.wait_ge(w_low, 6)

            def steady(s, u, front):
                gb, gm, gf, ub = s - 1, s, s + 1, 1 - u
                embed(gm, u, 0)
                embed(gm, u, 1)
                taps(gm, M, 0, 6)
                messages(gm, u, 0)
                messages(gm, u, 1)
                gates(gb, ub, 0)
                gates(gb, ub, 1)
                taps(gm, M, 6, 7)
                y_transpose(gb, 0)
                taps(gm, M, 7, NM)
                taps(gm, A, 0, 3)
                y_transpose(gb, 1)
                taps(gm, A, 3, 6)
                aggregate(gb, ub, 0)
                taps(gm, A, 6, 7)
                aggregate(gb, ub, 1)
                distances(gm, 0)
                distances(gm, 1)
                mlp1(gb, 0)
                distances(gm, 2)
                distances(gm, 3)
                taps(gm, A, 7, 8)
                mlp1(gb, 1)
                mlp2(gb, 0)
                taps(gm, A, 8, NP_)
                mlp2(gb, 1)
                nmp(gm, 0)
                taps(gm, B_, 0, 1)
                nmp(gm, 1)
                taps(gm, B_, 1, 2)
                if front:
                    conv1(gf, ub, 0)
                taps(gm, B_, 2, 3)
                if front:
                    conv1(gf, ub, 1)
                taps(gm, B_, 3, NR)

            def last(g, u):
                gates(g, u, 0)
                gates(g, u, 1)
                y_transpose(g, 0)
                y_transpose(g, 1)
                aggregate(g, u, 0)
                aggregate(g, u, 1)
                mlp1(g, 0)
                mlp1(g, 1)
                mlp2(g, 0)
                mlp2(g, 1)

            run(pe, prologue, steady, last)


_INS = ['x', 'adj', 'L0_gnn_w_se', 'L0_gnn_b_se', 'L0_gnn_conv1_w', 'L0_gnn_bn1_g', 'L0_gnn_bn1_b', 'L0_gnn_bn1_m',
        'L0_gnn_bn1_v', 'L0_gnn_conv2_w', 'L0_gnn_bn2_g', 'L0_gnn_bn2_b', 'L0_gnn_bn2_m', 'L0_gnn_bn2_v', 'L0_gnn_w_msg',
        'L0_gnn_b_msg', 'L0_gnn_w_ih', 'L0_gnn_b_ih', 'L0_gnn_w_hh', 'L0_gnn_b_hh', 'L1_gnn_eps', 'L1_gnn_W1', 'L1_gnn_b1',
        'L1_gnn_W2', 'L1_gnn_b2']


def kernel(**inputs):
    import numpy as _np
    import concourse.bacc as _bacc
    from concourse import mybir as _mybir
    from concourse.bass_utils import run_bass_kernel_spmd as _run

    nc = _bacc.Bacc("TRN2", target_bir_lowering=False, num_devices=1)
    arrays, aps = {}, {}
    for name, a in laid_out({n: inputs[n] for n in _INS}).items():
        arrays[f"in_{name}_dram"] = a
        aps[name] = nc.dram_tensor(f"in_{name}_dram", a.shape, _mybir.dt.from_np(a.dtype), kind="ExternalInput").ap()
    out = nc.dram_tensor("out_0_dram", (B, N, D), _mybir.dt.float32, kind="ExternalOutput").ap()
    gnn_kernel(nc, aps, out)
    r = _run(nc, [arrays], core_ids=[0])
    return r.results[0]["out_0_dram"]
```

```python
import concourse.bass as bass
from concourse import mybir
from contextlib import ExitStack
import numpy as np

B, N, D = 32, 256, 128
TAPS = 17
HID = 256
NSE = 3
EPS = 1e-5

GB = 4
GROUPS = B // GB
P = 128
PAR = N // P
T = N // PAR
PAIRS = GB // 2
COLS = GB * N
PC = COLS // PAIRS
BLK = PC // P
PAD = (TAPS // 2) // PAR
TL = T + 2 * PAD
NM, NP_, NR = (TAPS + 1) // 2, (TAPS + 1) // 2, TAPS // 2

SLOT = {("conv1", 0): 0}
for _name, _n in (("M", NM), ("A", NP_), ("B", NR), ("hid", 3), ("nmp", 3), ("conv", 3)):
    for _k in range(_n):
        SLOT[(_name, _k)] = len(SLOT)
NSLOT = len(SLOT)
S_M, S_A, S_B, S_GATE = (SLOT[(n, 0)] for n in ("M", "A", "B", "hid"))

(BN1_G, BN1_B, BN1_M, BN1_V, BN2_G, BN2_B, BN2_M, BN2_V,
 BIH, BHH, B1, BSE, EPS1) = 0, 1, 2, 3, 4, 5, 6, 7, 8, 11, 14, 16, 17
NVEC = 18

SROWS = 96
SQ_MASK, LIN_ONE, A_MUL, A_ADD, B_MUL, B_ADD = range(6)


def shape_constants():
    c = np.zeros((P, P + 6), np.float32)
    c[:, :P] = np.eye(P, dtype=np.float32)
    for q in range(3):
        for j in range(3):
            for i in range(NSE):
                r = 32 * q + NSE * j + i
                c[r, P + SQ_MASK] = j > 0
                c[r, P + LIN_ONE] = j == 0
                c[r, P + A_MUL] = (2.0, 0.0, 1.0)[j]
                c[r, P + A_ADD] = -1.0 if j == 1 and q != 0 else 0.0
                c[r, P + B_MUL] = (1.0, 1.0, 0.0)[j]
                c[r, P + B_ADD] = -1.0 if j == 2 and q != 2 else 0.0
    return c


def laid_out(a):
    f = {n: np.asarray(v) for n, v in a.items()}
    o = {}
    o["x"] = f["x"].reshape(GROUPS, GB, T, PAR, D).transpose(0, 4, 1, 3, 2)
    o["adj"] = f["adj"].reshape(GROUPS, GB, T, PAR, T, PAR).transpose(0, 4, 1, 5, 3, 2)
    se = np.zeros((P, SROWS), np.float32)
    bse = np.zeros((P,), np.float32)
    for q in range(3):
        for j in range(3):
            r = 32 * q + NSE * j
            se[:, r:r + NSE] = f["L0_gnn_w_se"].T
            bse[r:r + NSE] = f["L0_gnn_b_se"]
    bn = [f[f"L0_gnn_bn{k}_{v}"] for k in (1, 2) for v in "gbmv"]
    vec = np.stack(bn + list(f["L0_gnn_b_ih"].reshape(3, P)) + list(f["L0_gnn_b_hh"].reshape(3, P))
                   + list(f["L1_gnn_b1"].reshape(2, P)) + [bse, np.repeat(f["L1_gnn_eps"], P)], axis=1)
    o["first"] = np.concatenate([vec, f["L0_gnn_conv1_w"][:, :, 0].T, se,
                                ], axis=1)
    o["conv2"] = f["L0_gnn_conv2_w"].transpose(1, 2, 0)
    ih = f["L0_gnn_w_ih"].reshape(3, P, 2, P).transpose(3, 2, 0, 1)
    hh = f["L0_gnn_w_hh"].reshape(3, P, P).transpose(2, 0, 1)
    o["gates"] = np.concatenate([hh, ih[:, 1], ih[:, 0]], axis=1)
    o["later"] = np.concatenate([f["L0_gnn_w_msg"].T, f["L1_gnn_W1"],
                                 f["L1_gnn_W2"].reshape(2, P, D).transpose(1, 0, 2).reshape(P, 2 * D),
                                 np.tile(f["L0_gnn_b_msg"], (P, 1)), np.tile(f["L1_gnn_b2"], (P, 1))], axis=1)
    o["consts"] = shape_constants()
    return {n: np.ascontiguousarray(v) for n, v in o.items()}


def gnn_kernel(nc, t, out):
    fp32 = mybir.dt.float32
    f32r = mybir.dt.float32r
    ALU = mybir.AluOpType
    ACT = mybir.ActivationFunctionType

    x_v = t["x"].rearrange("g d b r t -> g d (b r t)")
    adj_v = t["adj"].rearrange("g m b r q n -> g m (b r q n)")
    out_v = out.rearrange("(g h b) (t r) d -> g h t b (r d)", h=PAIRS, b=GB // PAIRS, r=PAR)

    ctx = ExitStack()
    with ctx:
        def sb(name, shape, dt=fp32):
            return ctx.enter_context(nc.sbuf_tensor(name, shape, dt))

        def sem(name):
            return ctx.enter_context(nc.semaphore(name))

        cst = sb("cst", [P, P + 6])
        ident = cst[:, 0:P]
        first_w = sb("first_w", [P, NVEC + P + SROWS])
        vec = first_w[:, 0:NVEC]
        c1raw = first_w[:, NVEC:NVEC + P]
        seraw = first_w[:, NVEC + P:NVEC + P + SROWS]
        later_w = sb("later_w", [P, P + HID + 2 * D + 2 * P])
        wmsgT = later_w[:, 0:P]
        w1raw = later_w[:, P:P + HID]
        w2 = later_w[:, P + HID:P + HID + 2 * D].rearrange("p (f d) -> p f d", d=D)
        bmsg = later_w[:, P + HID + 2 * D:2 * P + HID + 2 * D]
        b2bc = later_w[:, 2 * P + HID + 2 * D:3 * P + HID + 2 * D]
        rs = sb("rs", [P, 2])
        one = sb("one", [P, 1])
        three = sb("three", [P, 1])
        bn = sb("bn", [P, 6])
        gbias = sb("gbias", [P, 4])
        sescale = sb("sescale", [SROWS, 1])
        minus_half = sb("minus_half", [P, BLK])
        epst = sb("epst", [P, 2, BLK])
        diag = sb("diag", [P, P])
        wh = sb("wh", [P, NSLOT, P], f32r)
        wl = sb("wl", [P, NSLOT, P], f32r)
        w1h = sb("w1h", [P, HID], f32r)
        w1l = sb("w1l", [P, HID], f32r)
        wseh = sb("wseh", [P, SROWS], f32r)
        wsel = sb("wsel", [P, SROWS], f32r)

        xv = [sb(f"xv{i}", [P, COLS]) for i in range(2)]
        xh = [sb(f"xh{i}", [P, COLS], f32r) for i in range(2)]
        xl = [sb(f"xl{i}", [P, COLS], f32r) for i in range(2)]
        sv = sb("sv", [SROWS, PAIRS, PC])
        sA = sb("sA", [SROWS, PAIRS, PC], f32r)
        sB = sb("sB", [SROWS, PAIRS, PC], f32r)
        msgh = sb("msgh", [P, PAIRS, BLK, D], f32r)
        msgl = sb("msgl", [P, PAIRS, BLK, D], f32r)
        adjT = sb("adjT", [P, GB, PAR, N])
        amat = sb("amat", [P, GB, PAR, N])
        mh = sb("mh", [P, GB, PAR, N], f32r)
        ml = sb("ml", [P, GB, PAR, N], f32r)
        nmph = sb("nmph", [P, COLS], f32r)
        nmpl = sb("nmpl", [P, COLS], f32r)
        h1 = sb("h1", [P, GB, PAR, TL])
        dv = sb("dv", [P, 2, GB, TL])
        sth = sb("sth", [P, 3, GB, TL], f32r)
        stl = sb("stl", [P, 3, GB, TL], f32r)
        usum = sb("usum", [P, GB, PAR, T])
        pre = usum
        xch = sb("xch", [P, GB, PAR, T], f32r)
        xcl = sb("xcl", [P, GB, PAR, T], f32r)
        gbuf = sb("gbuf", [P, 3, PAIRS, PC])
        tr, tz, ghn = (gbuf[:, i, :, :] for i in range(3))
        gwork = sb("gwork", [P, 2, PAIRS, PC])
        nn, xw = gwork[:, 0, :, :], gwork[:, 1, :, :]
        stats = sb("stats", [P, 2, PAIRS, BLK, 6])
        mv = sb("mv", [P, 2, PAIRS, BLK, 2])
        rstd = sb("rstd", [P, 2, PAIRS, BLK])
        xn = sb("xn", [P, PAIRS, BLK, D])
        msg = xn
        hh = sb("hh", [P, PAIRS, PC], f32r)
        hl = sb("hl", [P, PAIRS, PC], f32r)
        tail = sb("tail", [P, (HID // P + 1) * COLS])
        hid = tail[:, 0:HID // P * COLS].rearrange("p (h f n) -> p h f n", h=PAIRS, f=HID // P)
        ot = tail[:, HID // P * COLS:].rearrange("p (h k d) -> p h k d", h=PAIRS, k=BLK)

        c2raw = tail[:, 0:TAPS * P].rearrange("p (k o) -> p k o", k=TAPS)
        msum = gwork[:, :, :, :].rearrange("p a h n -> p (a h n)")[:, 0:NM * P].rearrange("p (k o) -> p k o", k=NM)
        graw = gbuf[:, :, :, :].rearrange("p a h n -> p (a h n)")[:, 0:9 * P].rearrange("p (k o) -> p k o", k=9)

        fb = [ctx.enter_context(nc.psum_tensor(f"front{i}", [P, PC], fp32)) for i in range(2)]
        bb = [ctx.enter_context(nc.psum_tensor(f"back{i}", [P, PC], fp32)) for i in range(3)]
        cb = [ctx.enter_context(nc.psum_tensor(f"conv{i}", [P, PC], fp32)) for i in range(3)]

        count = {}

        def stage(name, per_group):
            count[name] = (sem(name), per_group)
            return name

        X_LOADED = stage("x_loaded", 16)
        ADJ_LOADED = stage("adj_loaded", 16)
        STORED = [stage(f"out{h}_stored", 16) for h in range(PAIRS)]
        XH_READY = stage("xh_ready", 2)
        XL_READY = stage("xl_ready", 2)
        C1_FULL = stage("conv1_full", 2)
        H1_READY = stage("h1_ready", 2)
        DV_READY = stage("h1_diff_ready", 2)
        STH_READY = stage("stream_high_ready", 3)
        ST_READY = [stage(f"stream{n}_ready", 1) for n in "MAB"]
        CONV_FULL = [stage(f"conv{n}_full", 1) for n in "MAB"]
        U_READY = stage("usum_ready", 2)
        XSUM_READY = stage("xconv_sum_ready", 2)
        PRE_READY = stage("pre_ready", 2)
        XCH_READY = stage("xconv_high_ready", 2)
        XCL_READY = stage("xconv_low_ready", 2)
        S_FULL = stage("se_full", 2)
        SV_READY = stage("sv_ready", 2)
        SW_READY = stage("sw_ready", 2)
        SHI_READY = stage("s_high_ready", 2)
        SLO_READY = stage("s_low_ready", 2)
        MSG_FULL = stage("msg_full", 2)
        MSUM_READY = stage("msg_sum_ready", 2)
        MSGH_READY = stage("msg_high_ready", 2)
        MSG_READY = stage("msg_ready", 2)
        DIST_FULL = stage("dist_full", 4)
        E_READY = stage("exp_ready", 4)
        A_READY = stage("a_ready", 4)
        AH_READY = stage("a_high_ready", 4)
        AL_READY = stage("a_low_ready", 4)
        ADJE_READY = stage("adjT_eps_ready", 4)
        ADJH_READY = stage("adj_high_ready", 4)
        ADJL_READY = stage("adj_low_ready", 4)
        NMP_FULL = stage("nmp_full", 2)
        NH_READY = stage("nmp_high_ready", 2)
        NL_READY = stage("nmp_low_ready", 2)
        R_FULL = stage("gate_r_full", 2)
        HN_FULL = stage("gate_hn_full", 2)
        IN_FULL = stage("gate_in_full", 2)
        Z_FULL = stage("gate_z_full", 2)
        TR_READY = stage("tr_ready", 2)
        GHN_READY = stage("ghn_ready", 2)
        T1_READY = stage("t1_ready", 2)
        T2_READY = stage("t2_ready", 2)
        N_READY = stage("n_ready", 2)
        TZ_READY = stage("tz_ready", 2)
        XW_READY = stage("x_weight_ready", 2)
        XWX_READY = stage("weighted_x_ready", 2)
        F_READY = stage("f_ready", 2)
        Y2_READY = stage("y2_ready", 2)
        Y_FULL = stage("y_full", 2)
        STATS = [stage(f"stats{k}_ready", 2) for k in (1, 2)]
        MV = [stage(f"mv{k}_ready", 2) for k in (1, 2)]
        VE = [stage(f"var_eps{k}_ready", 2) for k in (1, 2)]
        RSTD = [stage(f"rstd{k}_ready", 2) for k in (1, 2)]
        XN_READY = stage("xn_ready", 2)
        XNH_READY = stage("xn_high_ready", 2)
        XNL_READY = stage("xn_low_ready", 2)
        XNB_READY = stage("xnb_ready", 2)
        AGG_FULL = stage("agg_full", 2)
        HH_READY = stage("h_high_ready", 2)
        HL_READY = stage("h_low_ready", 2)
        W1_FULL = stage("w1_full", 4)
        HID_READY = stage("hid_ready", 4)
        W2_FULL = stage("w2_full", 2)
        V_READY = stage("v_ready", 2)
        OT_READY = stage("out_ready", 2)

        consts_loaded = sem("consts_loaded")
        first_loaded = sem("first_loaded")
        x_pair0_loaded = sem("x_pair0_loaded")
        conv2_loaded = sem("conv2_loaded")
        gates_loaded = sem("gates_loaded")
        later_loaded = sem("later_loaded")
        exponent_set = sem("exponent_set")
        pads_zeroed = sem("pads_zeroed")
        bn_var_ready = sem("bn_var_ready")
        bn_rsqrt_ready = sem("bn_rsqrt_ready")
        bn_ready = sem("bn_ready")
        prep_chain = sem("prep_chain")
        tap_sums = sem("tap_sums")
        w_high = sem("w_high")
        w_low = sem("w_low")

        def wait(eng, name, g, j):
            s, per = count[name]
            v = g * per + j
            if not (isinstance(v, int) and v <= 0):
                eng.wait_ge(s, v)

        def done(ins, name):
            s, per = count[name]
            ins.then_inc(s, 16 if per == 16 else 1)

        def blocks(ap):
            return ap.rearrange("p (k c) -> p k c", c=P)

        def flat(ap):
            return ap.rearrange("p b r n -> p (b r n)")

        def full(ap):
            return ap.bitcast(fp32)

        def cols(h):
            return slice(h * PC, (h + 1) * PC)

        WHOLE = "whole"
        LAST_ITEMS = ((0, WHOLE), (1, 0), (1, 1))

        def halved(c):
            return c in (0, 1)

        def item(h, c):
            return h + (c if halved(c) else 0)

        def part(c):
            return slice(c * N, (c + 1) * N) if halved(c) else slice(0, PC)

        def part_cols(h, c):
            return slice(h * PC + part(c).start, h * PC + part(c).stop)

        def part_blocks(c):
            return range(c * BLK // 2, (c + 1) * BLK // 2) if halved(c) else range(BLK)

        def part_graphs(h, c):
            return slice(2 * h + c, 2 * h + c + 1) if halved(c) else slice(2 * h, 2 * h + 2)

        Y_TILE, AGG_TILE, HID_TILE, OUT_TILE = 8, 10, 12, 16
        LAST_BANKS = bb + cb + fb
        LAST_TILES = ([("gate", i, k) for i in (0, 1) for k in range(4)] + [("y", 0, 0)]
                      + [("gate", 2, k) for k in range(4)] + [("y", 1, 0), ("y", 2, 0)]
                      + [("agg", i, 0) for i in range(3)] + [("hid", i, k) for i in (0, 1) for k in range(2)]
                      + [("out", 0, 0), ("hid", 2, 0), ("hid", 2, 1), ("out", 1, 0), ("out", 2, 0)])

        def bank(kind, h, c, k=0):
            if c is None:
                n = {"gate": 4 * h + k, "y": Y_TILE + h, "agg": AGG_TILE + h, "hid": HID_TILE + 2 * h + k,
                     "out": OUT_TILE + h}[kind]
                return bb[n % 3][:, part(c)]
            return LAST_BANKS[LAST_TILES.index((kind, item(h, c), k)) % 8][:, part(c)]

        def run(eng, prologue, steady, last):
            prologue()
            steady(1, 1, True)
            with eng.Fori(0, (GROUPS - 4) // 2) as i:
                steady(i * 2 + 2, 0, True)
                steady(i * 2 + 3, 1, True)
            steady(GROUPS - 2, 0, True)
            steady(GROUPS - 1, 1, False)
            last(GROUPS - 1, (GROUPS - 1) % 2)

        block = ctx.enter_context(nc.Block())

        @block.sync
        def _(sp):
            def load_x(g, u):
                done(sp.dma_start(xv[u][:, :], x_v[g, :, :]), X_LOADED)

            def load_adj(g):
                done(sp.dma_start(flat(adjT[:, :, :, :]), adj_v[g, :, :]), ADJ_LOADED)

            def store(g, h, c=None):
                wait(sp, OT_READY, g, item(h, c) + 1)
                q = slice(part_blocks(c).start, part_blocks(c).stop)
                dst = out_v[g, h, :, c:c + 1, :] if halved(c) else out_v[g, h, :, :, :]
                done(sp.dma_start(dst, ot[:, h, q, :].rearrange("p (b r) d -> p b (r d)", r=PAR)), STORED[h])

            def prologue():
                sp.dma_start(first_w[:, :], t["first"]).then_inc(first_loaded, 16)
                sp.dma_start(xv[0][:, cols(0)], x_v[0, :, cols(0)]).then_inc(x_pair0_loaded, 16)
                done(sp.dma_start(xv[0][:, cols(1)], x_v[0, :, cols(1)]), X_LOADED)
                sp.dma_start(c2raw, t["conv2"]).then_inc(conv2_loaded, 16)
                sp.dma_start(later_w[:, :], t["later"]).then_inc(later_loaded, 16)
                load_adj(0)
                sp.dma_start(graw, t["gates"]).then_inc(gates_loaded, 16)
                wait(sp, X_LOADED, 0, 16)
                load_x(1, 1)
                wait(sp, ADJL_READY, 0, 4)
                load_adj(1)

            def steady(s, u, front):
                gb = s - 1
                if front:
                    wait(sp, XWX_READY, gb, 2)
                    load_x(s + 1, 1 - u)
                store(gb, 0)
                store(gb, 1)
                if front:
                    wait(sp, ADJL_READY, s, 4)
                    load_adj(s + 1)

            def last(g, u):
                for h, c in LAST_ITEMS:
                    store(g, h, c)
                wait(sp, STORED[0], g, 16)
                wait(sp, STORED[1], g, 32)

            run(sp, prologue, steady, last)

        @block.gpsimd
        def _(pool):
            def differences(g):
                wait(pool, H1_READY, g, 2)
                wait(pool, ST_READY[1], g - 1, 1)
                done(pool.tensor_tensor(dv[:, 0, :, :], h1[:, :, 0, :], h1[:, :, 1, :], ALU.subtract), DV_READY)
                wait(pool, ST_READY[2], g - 1, 1)
                done(pool.tensor_tensor(dv[:, 1, :, 0:TL - 1], h1[:, :, 0, 1:TL], h1[:, :, 1, 0:TL - 1],
                                        ALU.subtract), DV_READY)

            def rsqrt(k, g, h, c=None):
                q = slice(part_blocks(c).start, part_blocks(c).stop)
                wait(pool, MV[k], g, item(h, c) + 1)
                done(pool.tensor_tensor(rstd[:, k, h, q], mv[:, k, h, q, 1], epst[:, k, q], ALU.add), VE[k])
                wait(pool, VE[k], g, item(h, c) + 1)
                done(pool.tensor_tensor(rstd[:, k, h, q], rstd[:, k, h, q], minus_half[:, q], ALU.pow), RSTD[k])

            def residual(g, u, h, c=None):
                wait(pool, XW_READY, g, item(h, c) + 1)
                done(pool.tensor_tensor(xw[:, h, part(c)], xw[:, h, part(c)], xv[u][:, part_cols(h, c)], ALU.mult),
                     XWX_READY)

            def add_b2(g, h, c=None):
                q = slice(part_blocks(c).start, part_blocks(c).stop)
                wait(pool, XN_READY, g, item(h, c) + 1)
                wait(pool, STORED[h], g - 1, 16)
                done(pool.tensor_tensor(ot[:, h, q, :], xn[:, h, q, :],
                                        b2bc.unsqueeze(1).to_broadcast([P, len(part_blocks(c)), D]), ALU.add), XNB_READY)

            def mask(g, b):
                wait(pool, E_READY, g, b + 1)
                wait(pool, ADJ_LOADED, g, 16)
                done(pool.tensor_tensor(amat[:, b, :, :], amat[:, b, :, :], adjT[:, b, :, :], ALU.mult),
                     A_READY)

            def add_diagonal(g, b):
                a = adjT[:, b, :, :].rearrange("p r n -> p (r n)")
                dg = bass.AP(a.tensor, a.offset, [a.ap[0], [N + P, PAR], [1, P]])
                wait(pool, A_READY, g, b + 1)
                done(pool.tensor_tensor(dg, dg, diag[:, :].unsqueeze(1).to_broadcast([P, PAR, P]), ALU.add), ADJE_READY)

            def adj_low(g, b):
                wait(pool, ADJH_READY, g, b + 1)
                done(pool.tensor_tensor(ml[:, b, :, :], adjT[:, b, :, :], full(mh[:, b, :, :]), ALU.subtract),
                     ADJL_READY)

            def prologue():
                pool.memset(minus_half[:, :], -0.5).then_inc(exponent_set, 1)
                pool.memset(one[:, :], 1.0)
                pool.memset(three[:, :], 3.0)
                pool.memset(h1[:, :, :, :], 0.0).then_inc(pads_zeroed, 1)
                pool.memset(dv[:, :, :, :], 0.0).then_inc(pads_zeroed, 1)
                pool.memset(epst[:, 0, :], 4 * EPS).then_inc(pads_zeroed, 1)
                pool.memset(epst[:, 1, :], EPS).then_inc(pads_zeroed, 1)
                pool.wait_ge(exponent_set, 1)
                pool.wait_ge(bn_var_ready, 1)
                pool.tensor_tensor(rs[:, :], rs[:, :], minus_half[:, 0:2], ALU.pow).then_inc(bn_rsqrt_ready, 1)
                pool.wait_ge(pads_zeroed, 4)
                differences(0)
                for b in range(GB):
                    mask(0, b)
                pool.wait_ge(bn_ready, 3)
                for b in range(GB):
                    add_diagonal(0, b)
                differences(1)
                for b in range(GB):
                    adj_low(0, b)

            def steady(s, u, front):
                gb, gm = s - 1, s
                residual(gb, 1 - u, 0)
                residual(gb, 1 - u, 1)
                rsqrt(0, gb, 0)
                rsqrt(0, gb, 1)
                add_b2(gb, 0)
                add_b2(gb, 1)
                for b in range(GB):
                    mask(gm, b)
                rsqrt(1, gb, 0)
                rsqrt(1, gb, 1)
                for b in range(GB):
                    add_diagonal(gm, b)
                if front:
                    differences(s + 1)
                for b in range(GB):
                    adj_low(gm, b)

            def last(g, u):
                residual(g, u, 0, WHOLE)
                residual(g, u, 1, 0)
                rsqrt(0, g, 0, WHOLE)
                residual(g, u, 1, 1)
                rsqrt(0, g, 1, 0)
                rsqrt(0, g, 1, 1)
                for h, c in LAST_ITEMS:
                    add_b2(g, h, c)
                for h, c in LAST_ITEMS:
                    rsqrt(1, g, h, c)

            run(pool, prologue, steady, last)

        @block.scalar
        def _(act):
            def high(dst, src, name):
                done(act.activation(dst, src, ACT.Copy), name)

            def x_high(g, u):
                wait(act, X_LOADED, g, 16)
                for h in range(PAIRS):
                    high(xh[u][:, cols(h)], xv[u][:, cols(h)], XH_READY)

            def h1_out(g, h):
                if h == 0:
                    wait(act, DV_READY, g - 1, 2)
                    wait(act, ST_READY[0], g - 1, 1)
                wait(act, C1_FULL, g, h + 1)
                done(act.activation(h1[:, 2 * h:2 * h + 2, :, PAD:PAD + T].rearrange("p b r t -> p (b r) t"),
                                    blocks(cb[h][:, :]), ACT.Relu, bias=bn[:, 2:3], scale=bn[:, 0:1]), H1_READY)

            def se_values(g, h):
                wait(act, S_FULL, g, h + 1)
                done(act.activation(sv[:, h, :], fb[h][0:SROWS, :], ACT.Identity,
                                    bias=sescale[:, 0:1], scale=cst[0:SROWS, P + SQ_MASK:P + SQ_MASK + 1]), SV_READY)

            def se_high(g, h):
                wait(act, SW_READY, g, h + 1)
                act.activation(sA[:, h, :], sv[:, h, :], ACT.Identity,
                               bias=cst[0:SROWS, P + A_ADD:P + A_ADD + 1], scale=cst[0:SROWS, P + A_MUL:P + A_MUL + 1])
                done(act.activation(sB[:, h, :], sv[:, h, :], ACT.Identity,
                                    bias=cst[0:SROWS, P + B_ADD:P + B_ADD + 1],
                                    scale=cst[0:SROWS, P + B_MUL:P + B_MUL + 1]), SHI_READY)

            def exps(g, b):
                wait(act, DIST_FULL, g, b + 1)
                done(act.activation(amat[:, b, :, :].rearrange("p r n -> p (r n)"), fb[b % 2][:, :], ACT.Exp), E_READY)

            def msg_high(g, h):
                wait(act, MSUM_READY, g, h + 1)
                done(act.activation(msgh[:, h, :, :], msg[:, h, :, :], ACT.Relu), MSGH_READY)

            def a_high(g, b):
                wait(act, A_READY, g, b + 1)
                high(mh[:, b, :, :], amat[:, b, :, :], AH_READY)

            def adj_high(g, b):
                wait(act, NMP_FULL, g, b // 2 + 1)
                wait(act, ADJE_READY, g, b + 1)
                high(mh[:, b, :, :], adjT[:, b, :, :], ADJH_READY)

            def xn_high(g, h, c=None):
                wait(act, XN_READY, g, item(h, c) + 1)
                high(hh[:, h, part(c)], xn[:, h, :, :].rearrange("p k d -> p (k d)")[:, part(c)], XNH_READY)

            def nmp_high(g, h):
                wait(act, NMP_FULL, g, h + 1)
                high(nmph[:, cols(h)], fb[h][:, :], NH_READY)

            def gates(g, h, c=None):
                wait(act, HN_FULL, g, item(h, c) + 1)
                done(act.activation(ghn[:, h, part(c)], bank("gate", h, c, 1), ACT.Identity,
                                    bias=gbias[:, 2:3], scale=0.5), GHN_READY)
                wait(act, R_FULL, g, item(h, c) + 1)
                done(act.activation(tr[:, h, part(c)], bank("gate", h, c, 0), ACT.Tanh,
                                    bias=gbias[:, 0:1], scale=0.5), TR_READY)
                wait(act, Z_FULL, g, item(h, c) + 1)
                done(act.activation(tz[:, h, part(c)], bank("gate", h, c, 2), ACT.Tanh,
                                    bias=gbias[:, 1:2], scale=0.5), TZ_READY)
                wait(act, TZ_READY, g, item(h, c) + 1)
                done(act.activation(xw[:, h, part(c)], tz[:, h, part(c)], ACT.Identity, bias=three[:, 0:1]), XW_READY)
                act.activation(tz[:, h, part(c)], tz[:, h, part(c)], ACT.Identity, bias=one[:, 0:1], scale=-1.0)
                wait(act, T2_READY, g, item(h, c) + 1)
                done(act.activation(nn[:, h, part(c)], ghn[:, h, part(c)], ACT.Tanh, bias=gbias[:, 3:4]), N_READY)

            def xconv_high(g, par):
                wait(act, PRE_READY, g, par + 1)
                high(xch[:, :, par, :], pre[:, :, par, :], XCH_READY)

            def h_high(g, h, c=None):
                wait(act, AGG_FULL, g, item(h, c) + 1)
                high(hh[:, h, part(c)], bank("agg", h, c), HH_READY)

            def hidden(g, h, c=None):
                for f in range(2):
                    wait(act, W1_FULL, g, 2 * item(h, c) + f + 1)
                    done(act.activation(hid[:, h, f, part(c)], bank("hid", h, c, f), ACT.Relu,
                                        bias=vec[:, B1 + f:B1 + f + 1]), HID_READY)

            def prologue():
                act.dma_start(cst[:, :], t["consts"]).then_inc(consts_loaded, 16)
                act.wait_ge(first_loaded, 16)
                act.activation(wh[:, 0, :], c1raw, ACT.Copy)
                act.activation(wseh[:, :], seraw, ACT.Copy).then_inc(w_high, 1)
                act.wait_ge(x_pair0_loaded, 16)
                high(xh[0][:, cols(0)], xv[0][:, cols(0)], XH_READY)
                wait(act, X_LOADED, 0, 16)
                high(xh[0][:, cols(1)], xv[0][:, cols(1)], XH_READY)
                act.wait_ge(pads_zeroed, 4)
                act.wait_ge(bn_ready, 1)
                h1_out(0, 0)
                act.wait_ge(tap_sums, 1)
                act.activation(wh[:, S_M:S_M + 3, :], msum[:, 0:3, :], ACT.Copy).then_inc(w_high, 1)
                h1_out(0, 1)
                for k in (3, 6):
                    act.wait_ge(tap_sums, k // 3 + 1)
                    act.activation(wh[:, S_M + k:S_M + k + 3, :], msum[:, k:k + 3, :], ACT.Copy).then_inc(w_high, 1)
                act.wait_ge(bn_ready, 3)
                se_values(0, 0)
                se_values(0, 1)
                act.activation(wh[:, S_A:S_A + NP_, :], c2raw[:, 0:TAPS:2, :], ACT.Copy).then_inc(w_high, 1)
                se_high(0, 0)
                se_high(0, 1)
                act.activation(wh[:, S_B:S_B + NR, :], c2raw[:, 1:TAPS:2, :], ACT.Copy).then_inc(w_high, 1)
                msg_high(0, 0)
                msg_high(0, 1)
                for b in range(GB):
                    exps(0, b)
                a_high(0, 0)
                a_high(0, 1)
                x_high(1, 1)
                a_high(0, 2)
                a_high(0, 3)
                act.wait_ge(gates_loaded, 16)
                act.activation(wh[:, S_GATE:S_GATE + 9, :], graw, ACT.Copy).then_inc(w_high, 1)
                act.activation(w1h[:, :], w1raw, ACT.Copy).then_inc(w_high, 1)
                xconv_high(0, 0)
                nmp_high(0, 0)
                h1_out(1, 0)
                h1_out(1, 1)
                nmp_high(0, 1)
                for b in range(GB):
                    adj_high(0, b)
                xconv_high(0, 1)

            def steady(s, u, front):
                gb, gm, gf = s - 1, s, s + 1
                se_values(gm, 0)
                se_values(gm, 1)
                se_high(gm, 0)
                se_high(gm, 1)
                msg_high(gm, 0)
                msg_high(gm, 1)
                gates(gb, 0)
                gates(gb, 1)
                if front:
                    x_high(gf, 1 - u)
                xn_high(gb, 0)
                xn_high(gb, 1)
                exps(gm, 0)
                exps(gm, 1)
                h_high(gb, 0)
                h_high(gb, 1)
                exps(gm, 2)
                exps(gm, 3)
                hidden(gb, 0)
                a_high(gm, 0)
                a_high(gm, 1)
                hidden(gb, 1)
                a_high(gm, 2)
                a_high(gm, 3)
                xconv_high(gm, 0)
                if front:
                    h1_out(gf, 0)
                nmp_high(gm, 0)
                if front:
                    h1_out(gf, 1)
                    nmp_high(gm, 1)
                    for b in range(GB):
                        adj_high(gm, b)
                    xconv_high(gm, 1)
                else:
                    xconv_high(gm, 1)
                    nmp_high(gm, 1)
                    for b in range(GB):
                        adj_high(gm, b)

            def last(g, u):
                for h, c in LAST_ITEMS:
                    gates(g, h, c)
                for h, c in LAST_ITEMS:
                    xn_high(g, h, c)
                for h, c in LAST_ITEMS:
                    h_high(g, h, c)
                for h, c in LAST_ITEMS:
                    hidden(g, h, c)

            run(act, prologue, steady, last)

        @block.vector
        def _(dve):
            def low(dst, src, hi, name):
                done(dve.tensor_tensor(dst, src, full(hi), ALU.subtract), name)

            def x_low(g, u, h):
                wait(dve, XH_READY, g, h + 1)
                low(xl[u][:, cols(h)], xv[u][:, cols(h)], xh[u][:, cols(h)], XL_READY)

            def split(g, st):
                src = (h1[:, :, 1, :], dv[:, 0, :, :], dv[:, 1, :, :])[st]
                if st == 0:
                    wait(dve, H1_READY, g, 2)
                else:
                    wait(dve, DV_READY, g, st)
                wait(dve, CONV_FULL[st], g - 1, 1)
                done(dve.tensor_copy(sth[:, st, :, :], src), STH_READY)
                wait(dve, STH_READY, g, st + 1)
                low(stl[:, st, :, :], src, sth[:, st, :, :], ST_READY[st])

            def se_rows(g, h):
                wait(dve, SV_READY, g, h + 1)
                done(dve.scalar_tensor_tensor(sv[:, h, :], fb[h][0:SROWS, :], vec[0:SROWS, BSE:BSE + 1], sv[:, h, :],
                                              ALU.add, ALU.mult), SW_READY)

            def se_low(g, h):
                wait(dve, SHI_READY, g, h + 1)
                dve.scalar_tensor_tensor(sA[0:32, h, :], sv[0:32, h, :], cst[0:32, P + A_MUL:P + A_MUL + 1],
                                         full(sA[0:32, h, :]), ALU.mult, ALU.subtract)
                done(dve.scalar_tensor_tensor(sB[64:96, h, :], sv[64:96, h, :], cst[64:96, P + B_MUL:P + B_MUL + 1],
                                              full(sB[64:96, h, :]), ALU.mult, ALU.subtract), SLO_READY)

            def messages(g, h):
                wait(dve, MSG_FULL, g, h + 1)
                wait(dve, NMP_FULL, g - 1, h + 1)
                done(dve.tensor_tensor(msg[:, h, :, :], blocks(fb[h][:, :]),
                                       bmsg.unsqueeze(1).to_broadcast([P, BLK, D]), ALU.add), MSUM_READY)

            def msg_low(g, h):
                wait(dve, MSGH_READY, g, h + 1)
                done(dve.scalar_tensor_tensor(msgl[:, h, :, :], msg[:, h, :, :], 0.0, full(msgh[:, h, :, :]),
                                              ALU.max, ALU.subtract), MSG_READY)

            def a_low(g, b):
                wait(dve, AH_READY, g, b + 1)
                low(ml[:, b, :, :], amat[:, b, :, :], mh[:, b, :, :], AL_READY)

            def nmp_low(g, h):
                wait(dve, NH_READY, g, h + 1)
                low(nmpl[:, cols(h)], fb[h][:, :], nmph[:, cols(h)], NL_READY)

            def shared_sum(g, u, par):
                wait(dve, CONV_FULL[0], g, 1)
                xs = xv[u][:, :].rearrange("p (b r t) -> p b r t", b=GB, r=PAR)
                m = cb[0][:, :].rearrange("p (b t) -> p b t", t=T)
                done(dve.scalar_tensor_tensor(usum[:, :, par, :], m, bn[:, 3:4], xs[:, :, par, :], ALU.mult, ALU.add),
                     U_READY)

            def pre_sum(g, par):
                wait(dve, CONV_FULL[1 + par], g, 1)
                wait(dve, U_READY, g, par + 1)
                done(dve.scalar_tensor_tensor(pre[:, :, par, :], cb[1 + par][:, :].rearrange("p (b t) -> p b t", t=T),
                                              bn[:, 3:4], usum[:, :, par, :], ALU.mult, ALU.add), XSUM_READY)
                wait(dve, XSUM_READY, g, par + 1)
                done(dve.tensor_scalar(pre[:, :, par, :], pre[:, :, par, :], bn[:, 5:6], 0.0, ALU.add, ALU.max), PRE_READY)

            def xconv_low(g, par):
                wait(dve, XCH_READY, g, par + 1)
                low(xcl[:, :, par, :], pre[:, :, par, :], xch[:, :, par, :], XCL_READY)

            def gates(g, u, h, c=None):
                wait(dve, GHN_READY, g, item(h, c) + 1)
                wait(dve, TR_READY, g, item(h, c) + 1)
                done(dve.scalar_tensor_tensor(ghn[:, h, part(c)], tr[:, h, part(c)], 1.0, ghn[:, h, part(c)],
                                              ALU.add, ALU.mult), T1_READY)
                wait(dve, IN_FULL, g, item(h, c) + 1)
                wait(dve, T1_READY, g, item(h, c) + 1)
                done(dve.tensor_tensor(ghn[:, h, part(c)], bank("gate", h, c, 3), ghn[:, h, part(c)], ALU.add), T2_READY)

            def gates_end(g, h, c=None):
                wait(dve, N_READY, g, item(h, c) + 1)
                done(dve.tensor_tensor(tr[:, h, part(c)], tz[:, h, part(c)], nn[:, h, part(c)], ALU.mult), F_READY)
                wait(dve, XWX_READY, g, item(h, c) + 1)
                wait(dve, F_READY, g, item(h, c) + 1)
                done(dve.tensor_tensor(tr[:, h, part(c)], tr[:, h, part(c)], xw[:, h, part(c)], ALU.add), Y2_READY)

            def norm_stats(k, g, h, c, src):
                for q in part_blocks(c):
                    last = dve.bn_stats(stats[:, k, h, q, :], src(q))
                done(last, STATS[k])
                wait(dve, STATS[k], g, item(h, c) + 1)
                dve.nop(nofuse=True)
                for q in part_blocks(c):
                    last = dve.bn_aggr(mv[:, k, h, q, :], stats[:, k, h, q, :])
                done(last, MV[k])

            def norm_apply(k, g, h, c, src, dst, ready):
                wait(dve, RSTD[k], g, item(h, c) + 1)
                for q in part_blocks(c):
                    last = dve.tensor_scalar(dst(q), src(q), mv[:, k, h, q, 0:1], rstd[:, k, h, q:q + 1],
                                             ALU.subtract, ALU.mult)
                done(last, ready)

            def y_block(h, c):
                tile, q0 = bank("y", h, c), part_blocks(c).start
                return lambda q: tile[:, (q - q0) * P:(q - q0 + 1) * P]

            def y_stats(g, h, c=None):
                wait(dve, Y_FULL, g, item(h, c) + 1)
                norm_stats(0, g, h, c, y_block(h, c))

            def y_apply(g, h, c=None):
                norm_apply(0, g, h, c, y_block(h, c), lambda q: xn[:, h, q, :], XN_READY)

            def xn_low(g, h, c=None):
                wait(dve, XNH_READY, g, item(h, c) + 1)
                low(hl[:, h, part(c)], xn[:, h, :, :].rearrange("p k d -> p (k d)")[:, part(c)], hh[:, h, part(c)], XNL_READY)

            def h_low(g, h, c=None):
                wait(dve, HH_READY, g, item(h, c) + 1)
                low(hl[:, h, part(c)], bank("agg", h, c), hh[:, h, part(c)], HL_READY)

            def out_stats(g, h, c=None):
                wait(dve, W2_FULL, g, item(h, c) + 1)
                wait(dve, XNB_READY, g, item(h, c) + 1)
                row = ot[:, h, :, :].rearrange("p k d -> p (k d)")[:, part(c)]
                done(dve.tensor_tensor(row, bank("out", h, c), row, ALU.add), V_READY)
                wait(dve, V_READY, g, item(h, c) + 1)
                norm_stats(1, g, h, c, lambda q: ot[:, h, q, :])

            def out_apply(g, h, c=None):
                norm_apply(1, g, h, c, lambda q: ot[:, h, q, :], lambda q: ot[:, h, q, :], OT_READY)

            def prologue():
                n = [0]

                def link(ins):
                    n[0] += 1
                    ins.then_inc(prep_chain, 1)
                    dve.wait_ge(prep_chain, n[0])

                def w_low_part(dst, src, hi, k):
                    dve.wait_ge(w_high, k)
                    dve.tensor_tensor(dst, src, full(hi), ALU.subtract).then_inc(w_low, 1)

                dve.wait_ge(first_loaded, 16)
                dve.tensor_scalar(rs[:, 0:1], vec[:, BN1_V:BN1_V + 1], EPS, None, ALU.add)
                dve.tensor_scalar(rs[:, 1:2], vec[:, BN2_V:BN2_V + 1], EPS, None, ALU.add).then_inc(bn_var_ready, 1)
                dve.wait_ge(w_high, 1)
                dve.tensor_tensor(wsel[:, :], seraw, full(wseh[:, :]), ALU.subtract)
                w_low_part(wl[:, 0, :], c1raw, wh[:, 0, :], 1)
                dve.wait_ge(bn_rsqrt_ready, 1)
                for k in range(2):
                    c = 3 * k
                    link(dve.tensor_tensor(bn[:, c:c + 1], rs[:, k:k + 1], vec[:, 4 * k:4 * k + 1], ALU.mult))
                    link(dve.tensor_tensor(bn[:, c + 1:c + 2], bn[:, c:c + 1], vec[:, 4 * k + 2:4 * k + 3], ALU.mult))
                    ins = dve.tensor_tensor(bn[:, c + 2:c + 3], vec[:, 4 * k + 1:4 * k + 2], bn[:, c + 1:c + 2], ALU.subtract)
                ins.then_inc(bn_ready, 1)
                x_low(0, 0, 0)
                x_low(0, 0, 1)
                dve.wait_ge(consts_loaded, 16)
                link(dve.scalar_tensor_tensor(sescale[:, :], vec[0:SROWS, BSE:BSE + 1],
                                              cst[0:SROWS, P + SQ_MASK:P + SQ_MASK + 1],
                                              cst[0:SROWS, P + LIN_ONE:P + LIN_ONE + 1], ALU.mult, ALU.add))
                link(dve.tensor_tensor(gbias[:, 0:3], vec[:, BIH:BIH + 3], vec[:, BHH:BHH + 3], ALU.add))
                link(dve.tensor_scalar(gbias[:, 0:2], gbias[:, 0:2], 0.5, None, ALU.mult))
                dve.tensor_scalar(gbias[:, 2:3], vec[:, BHH + 2:BHH + 3], 0.5, None, ALU.mult)
                dve.tensor_copy(gbias[:, 3:4], vec[:, BIH + 2:BIH + 3]).then_inc(bn_ready, 1)
                dve.scalar_tensor_tensor(diag[:, :], ident, vec[:, EPS1:EPS1 + 1], ident,
                                         ALU.mult, ALU.add).then_inc(bn_ready, 1)
                dve.wait_ge(conv2_loaded, 16)
                for k in range(0, NM, 3):
                    n = min(3, NM - 1 - k)
                    ins = dve.tensor_tensor(msum[:, k:k + n, :], c2raw[:, 2 * k:2 * (k + n):2, :],
                                            c2raw[:, 2 * k + 1:2 * (k + n):2, :], ALU.add)
                    if n < 3:
                        ins = dve.tensor_copy(msum[:, NM - 1, :], c2raw[:, TAPS - 1, :])
                    ins.then_inc(tap_sums, 1)
                w_low_part(wl[:, S_M:S_M + 3, :], msum[:, 0:3, :], wh[:, S_M:S_M + 3, :], 2)
                split(0, 0)
                w_low_part(wl[:, S_M + 3:S_M + 6, :], msum[:, 3:6, :], wh[:, S_M + 3:S_M + 6, :], 3)
                w_low_part(wl[:, S_M + 6:S_M + NM, :], msum[:, 6:NM, :], wh[:, S_M + 6:S_M + NM, :], 4)
                se_rows(0, 0)
                se_rows(0, 1)
                w_low_part(wl[:, S_A:S_A + NP_, :], c2raw[:, 0:TAPS:2, :], wh[:, S_A:S_A + NP_, :], 5)
                split(0, 1)
                se_low(0, 0)
                dve.wait_ge(later_loaded, 16)
                messages(0, 0)
                messages(0, 1)
                se_low(0, 1)
                msg_low(0, 0)
                msg_low(0, 1)
                split(0, 2)
                w_low_part(wl[:, S_B:S_B + NR, :], c2raw[:, 1:TAPS:2, :], wh[:, S_B:S_B + NR, :], 6)
                shared_sum(0, 0, 0)
                shared_sum(0, 0, 1)
                a_low(0, 0)
                a_low(0, 1)
                x_low(1, 1, 0)
                x_low(1, 1, 1)
                a_low(0, 2)
                a_low(0, 3)
                pre_sum(0, 0)
                dve.wait_ge(gates_loaded, 16)
                w_low_part(wl[:, S_GATE:S_GATE + 9, :], graw, wh[:, S_GATE:S_GATE + 9, :], 7)
                w_low_part(w1l[:, :], w1raw, w1h[:, :], 8)
                nmp_low(0, 0)
                nmp_low(0, 1)
                split(1, 0)
                xconv_low(0, 0)
                pre_sum(0, 1)
                split(1, 1)
                xconv_low(0, 1)

            def steady(s, u, front):
                gb, gm, gf = s - 1, s, s + 1
                se_rows(gm, 0)
                se_rows(gm, 1)
                messages(gm, 0)
                messages(gm, 1)
                se_low(gm, 0)
                se_low(gm, 1)
                msg_low(gm, 0)
                msg_low(gm, 1)
                split(gm, 2)
                gates(gb, 1 - u, 0)
                gates_end(gb, 0)
                gates(gb, 1 - u, 1)
                y_stats(gb, 0)
                gates_end(gb, 1)
                y_apply(gb, 0)
                y_stats(gb, 1)
                xn_low(gb, 0)
                y_apply(gb, 1)
                shared_sum(gm, u, 0)
                xn_low(gb, 1)
                shared_sum(gm, u, 1)
                h_low(gb, 0)
                h_low(gb, 1)
                if front:
                    x_low(gf, 1 - u, 0)
                    x_low(gf, 1 - u, 1)
                a_low(gm, 0)
                a_low(gm, 1)
                pre_sum(gm, 0)
                out_stats(gb, 0)
                a_low(gm, 2)
                a_low(gm, 3)
                xconv_low(gm, 0)
                out_stats(gb, 1)
                nmp_low(gm, 0)
                if front:
                    out_apply(gb, 0)
                    nmp_low(gm, 1)
                    split(gf, 0)
                    out_apply(gb, 1)
                    pre_sum(gm, 1)
                    split(gf, 1)
                    xconv_low(gm, 1)
                else:
                    pre_sum(gm, 1)
                    out_apply(gb, 0)
                    xconv_low(gm, 1)
                    nmp_low(gm, 1)
                    out_apply(gb, 1)

            def last(g, u):
                gates(g, u, 0, WHOLE)
                gates_end(g, 0, WHOLE)
                gates(g, u, 1, 0)
                y_stats(g, 0, WHOLE)
                gates_end(g, 1, 0)
                gates(g, u, 1, 1)
                y_apply(g, 0, WHOLE)
                gates_end(g, 1, 1)
                y_stats(g, 1, 0)
                y_stats(g, 1, 1)
                xn_low(g, 0, WHOLE)
                y_apply(g, 1, 0)
                y_apply(g, 1, 1)
                xn_low(g, 1, 0)
                xn_low(g, 1, 1)
                for h, c in LAST_ITEMS:
                    h_low(g, h, c)
                out_stats(g, 0, WHOLE)
                out_stats(g, 1, 0)
                out_stats(g, 1, 1)
                for h, c in LAST_ITEMS:
                    out_apply(g, h, c)

            run(dve, prologue, steady, last)

        @block.tensor
        def _(pe):
            def products(bank, terms, first=True, last=True):
                todo = [(a, b) for (ah, al, bh, bl) in terms for (a, b) in ((ah, bh), (ah, bl), (al, bh))]
                for k, (a, b) in enumerate(todo):
                    ins = pe.matmul(bank, a, b, start=first and k == 0, stop=last and k == len(todo) - 1)
                return ins

            def weights(name, k):
                i = SLOT[(name, k)]
                return wh[:, i, :], wl[:, i, :]

            def taps(g, st, k0, k1):
                n = (NM, NP_, NR)[st]
                if k0 == 0:
                    wait(pe, ST_READY[st], g, 1)
                    if st == 2:
                        wait(pe, XSUM_READY, g - 1, 2)
                    else:
                        wait(pe, H1_READY, g, st + 1)
                bank = cb[st][:, :].rearrange("p (b t) -> p b t", t=T)
                for k in range(k0, k1):
                    ins = products(bank, [weights("MAB"[st], k) + (sth[:, st, :, k:k + T], stl[:, st, :, k:k + T])],
                                   first=k == 0, last=k == n - 1)
                if k1 == n:
                    done(ins, CONV_FULL[st])

            def conv1(g, u, h):
                wait(pe, U_READY, g - 1, 2) if h == 0 else wait(pe, XSUM_READY, g - 1, 1)
                wait(pe, XL_READY, g, h + 1)
                done(products(cb[h][:, :], [weights("conv1", 0) + (xh[u][:, cols(h)], xl[u][:, cols(h)])]), C1_FULL)

            def embed(g, u, h):
                wait(pe, NL_READY, g - 1, h + 1)
                wait(pe, XL_READY, g, h + 1)
                done(products(fb[h][0:SROWS, :], [(wseh[:, :], wsel[:, :], xh[u][:, cols(h)], xl[u][:, cols(h)])]), S_FULL)

            def messages(g, u, h):
                wait(pe, SW_READY, g, h + 1)
                for q in range(BLK):
                    ins = pe.matmul(fb[h][:, q * P:(q + 1) * P], xv[u][:, h * PC + q * P:h * PC + (q + 1) * P], wmsgT,
                                    start=True, stop=True)
                done(ins, MSG_FULL)

            def distances(g, b):
                if b < 2:
                    wait(pe, MSUM_READY, g, b + 1)
                else:
                    wait(pe, E_READY, g, b - 1)
                wait(pe, SLO_READY, g, b // 2 + 1)
                h, o = b // 2, (b % 2) * N
                for rm in range(PAR):
                    ins = pe.matmul(fb[b % 2][:, rm * N:(rm + 1) * N], sA[:, h, o + rm * P:o + (rm + 1) * P],
                                    sB[:, h, o:o + N], start=True, stop=True)
                done(ins, DIST_FULL)

            def gather(tile, c, lhs, rhs):
                for k, b in enumerate((c,) if halved(c) else range(2)):
                    ins = products(tile[:, k * N:(k + 1) * N], [lhs(b, rm) + rhs(b, rm) for rm in range(PAR)])
                return ins

            def nmp(g, h):
                wait(pe, E_READY, g, h + 3)
                wait(pe, MSG_READY, g, h + 1)
                wait(pe, AL_READY, g, 2 * h + 2)
                done(gather(fb[h], None, lambda b, rm: (msgh[:, h, 2 * b + rm, :], msgl[:, h, 2 * b + rm, :]),
                            lambda b, rm: (mh[:, 2 * h + b, rm, :], ml[:, 2 * h + b, rm, :])), NMP_FULL)

            def gates(g, u, h, c=None):
                n = part_cols(h, c)
                xx = (xh[u][:, n], xl[u][:, n])
                nm = (nmph[:, n], nmpl[:, n])
                xc = (xch[:, part_graphs(h, c), :, :].rearrange("p b r t -> p (b r t)"),
                      xcl[:, part_graphs(h, c), :, :].rearrange("p b r t -> p (b r t)"))
                r, hn, z, inn = (bank("gate", h, c, k) for k in range(4))
                i = item(h, c)
                if i == 0:
                    wait(pe, HID_READY, g - 1, 4)
                elif i == 2 or c is None:
                    wait(pe, GHN_READY, g, 1)
                wait(pe, NL_READY, g, h + 1)
                products(r, [weights("hid", 0) + xx, weights("nmp", 0) + nm], last=False)
                if i == 0:
                    wait(pe, V_READY, g - 1, 2)
                elif i == 2 or c is None:
                    wait(pe, TZ_READY, g, 1)
                done(products(hn, [weights("hid", 2) + xx]), HN_FULL)
                if i == 0:
                    wait(pe, XCL_READY, g, 2)
                done(products(r, [weights("conv", 0) + xc], first=False), R_FULL)
                if i == 2 or (i == 1 and c is None):
                    wait(pe, T2_READY, g, 1)
                done(products(z, [weights("hid", 1) + xx, weights("nmp", 1) + nm, weights("conv", 1) + xc]), Z_FULL)
                if c is None:
                    wait(pe, TR_READY, g, i + 1)
                elif i == 2:
                    wait(pe, TR_READY, g, 2)
                done(products(inn, [weights("nmp", 2) + nm, weights("conv", 2) + xc]), IN_FULL)

            def y_transpose(g, h, c=None):
                i = item(h, c)
                if c is None:
                    wait(pe, (GHN_READY, TZ_READY)[h], g, 2)
                else:
                    wait(pe, (TR_READY, GHN_READY, TZ_READY)[i], g, (1, 2, 2)[i])
                wait(pe, Y2_READY, g, i + 1)
                for k, q in enumerate(part_blocks(c)):
                    ins = pe.transpose(bank("y", h, c)[:, k * P:(k + 1) * P], tr[:, h, q * P:(q + 1) * P], ident)
                done(ins, Y_FULL)

            def aggregate(g, h, c=None):
                i = item(h, c)
                if c is not None:
                    wait(pe, (T2_READY, XN_READY, TR_READY)[i], g, (2, 1, 3)[i])
                elif h == 0:
                    wait(pe, T2_READY, g, 2)
                wait(pe, XNL_READY, g, i + 1)
                wait(pe, ADJL_READY, g, 2 * h + 2)
                block = lambda b, rm: slice((2 * b + rm) * P, (2 * b + rm + 1) * P)
                done(gather(bank("agg", h, c), c, lambda b, rm: (hh[:, h, block(b, rm)], hl[:, h, block(b, rm)]),
                            lambda b, rm: (mh[:, 2 * h + b, rm, :], ml[:, 2 * h + b, rm, :])), AGG_FULL)

            def mlp1(g, h, c=None):
                i = item(h, c)
                for f in range(2):
                    if c is None:
                        wait(pe, ((XN_READY, HL_READY), (HL_READY, HID_READY))[h][f], g, 2 - f)
                    else:
                        wait(pe, ((GHN_READY, TZ_READY), (T2_READY, XN_READY), (HL_READY, HL_READY))[i][f], g,
                             ((3, 3), (3, 2), (1, 2))[i][f])
                    wait(pe, HL_READY, g, i + 1)
                    done(products(bank("hid", h, c, f),
                                  [(w1h[:, f * P:(f + 1) * P], w1l[:, f * P:(f + 1) * P],
                                    hh[:, h, part(c)], hl[:, h, part(c)])]), W1_FULL)

            def mlp2(g, h, c=None):
                i = item(h, c)
                wait(pe, HID_READY, g, 2 * i + 2)
                if c is not None:
                    wait(pe, (XN_READY, HL_READY, HID_READY)[i], g, (3, 3, 1)[i])
                for k, q in enumerate(part_blocks(c)):
                    for f in range(2):
                        ins = pe.matmul(bank("out", h, c)[:, k * P:(k + 1) * P], hid[:, h, f, q * P:(q + 1) * P],
                                        w2[:, f, :], start=f == 0, stop=f == 1)
                done(ins, W2_FULL)

            M, A, B_ = 0, 1, 2

            def prologue():
                pe.wait_ge(w_low, 1)
                conv1(0, 0, 0)
                conv1(0, 0, 1)
                embed(0, 0, 0)
                embed(0, 0, 1)
                pe.wait_ge(w_low, 2)
                taps(0, M, 0, 3)
                pe.wait_ge(w_low, 3)
                taps(0, M, 3, 6)
                pe.wait_ge(later_loaded, 16)
                messages(0, 0, 0)
                messages(0, 0, 1)
                pe.wait_ge(w_low, 4)
                taps(0, M, 6, NM)
                pe.wait_ge(w_low, 5)
                taps(0, A, 0, 4)
                distances(0, 0)
                distances(0, 1)
                taps(0, A, 4, 6)
                distances(0, 2)
                distances(0, 3)
                taps(0, A, 6, NP_)
                pe.wait_ge(w_low, 6)
                taps(0, B_, 0, 3)
                nmp(0, 0)
                taps(0, B_, 3, 4)
                conv1(1, 1, 0)
                taps(0, B_, 4, 5)
                conv1(1, 1, 1)
                nmp(0, 1)
                taps(0, B_, 5, NR)
                pe.wait_ge(w_low, 8)

            def steady(s, u, front):
                gb, gm, gf, ub = s - 1, s, s + 1, 1 - u
                embed(gm, u, 0)
                embed(gm, u, 1)
                taps(gm, M, 0, 7)
                messages(gm, u, 0)
                messages(gm, u, 1)
                gates(gb, ub, 0)
                gates(gb, ub, 1)
                y_transpose(gb, 0)
                taps(gm, M, 7, NM)
                taps(gm, A, 0, 3)
                y_transpose(gb, 1)
                taps(gm, A, 3, 8)
                distances(gm, 0)
                distances(gm, 1)
                aggregate(gb, 0)
                taps(gm, A, 8, NP_)
                taps(gm, B_, 0, 1)
                aggregate(gb, 1)
                distances(gm, 2)
                distances(gm, 3)
                mlp1(gb, 0)
                taps(gm, B_, 1, 2)
                mlp1(gb, 1)
                mlp2(gb, 0)
                taps(gm, B_, 2, 3)
                mlp2(gb, 1)
                if front:
                    conv1(gf, ub, 0)
                nmp(gm, 0)
                if front:
                    conv1(gf, ub, 1)
                    taps(gm, B_, 3, 4)
                    nmp(gm, 1)
                    taps(gm, B_, 4, NR)
                else:
                    taps(gm, B_, 3, NR)
                    nmp(gm, 1)

            def last(g, u):
                gates(g, u, 0, WHOLE)
                gates(g, u, 1, 0)
                y_transpose(g, 0, WHOLE)
                gates(g, u, 1, 1)
                y_transpose(g, 1, 0)
                y_transpose(g, 1, 1)
                for h, c in LAST_ITEMS:
                    aggregate(g, h, c)
                mlp1(g, 0, WHOLE)
                mlp1(g, 1, 0)
                mlp2(g, 0, WHOLE)
                mlp1(g, 1, 1)
                mlp2(g, 1, 0)
                mlp2(g, 1, 1)

            run(pe, prologue, steady, last)


_INS = ['x', 'adj', 'L0_gnn_w_se', 'L0_gnn_b_se', 'L0_gnn_conv1_w', 'L0_gnn_bn1_g', 'L0_gnn_bn1_b', 'L0_gnn_bn1_m',
        'L0_gnn_bn1_v', 'L0_gnn_conv2_w', 'L0_gnn_bn2_g', 'L0_gnn_bn2_b', 'L0_gnn_bn2_m', 'L0_gnn_bn2_v', 'L0_gnn_w_msg',
        'L0_gnn_b_msg', 'L0_gnn_w_ih', 'L0_gnn_b_ih', 'L0_gnn_w_hh', 'L0_gnn_b_hh', 'L1_gnn_eps', 'L1_gnn_W1', 'L1_gnn_b1',
        'L1_gnn_W2', 'L1_gnn_b2']


def kernel(**inputs):
    import numpy as _np
    import concourse.bacc as _bacc
    from concourse import mybir as _mybir
    from concourse.bass_utils import run_bass_kernel_spmd as _run

    nc = _bacc.Bacc("TRN2", target_bir_lowering=False, num_devices=1)
    arrays, aps = {}, {}
    for name, a in laid_out({n: inputs[n] for n in _INS}).items():
        arrays[f"in_{name}_dram"] = a
        aps[name] = nc.dram_tensor(f"in_{name}_dram", a.shape, _mybir.dt.from_np(a.dtype), kind="ExternalInput").ap()
    out = nc.dram_tensor("out_0_dram", (B, N, D), _mybir.dt.float32, kind="ExternalOutput").ap()
    gnn_kernel(nc, aps, out)
    r = _run(nc, [arrays], core_ids=[0])
    return r.results[0]["out_0_dram"]
```
